# Optimizing a Trainium2 kernel written in Bass

```python
import numpy as np
import jax
import jax.numpy as jnp

def _softmax(x, axis=-1):
    return jax.nn.softmax(x, axis=axis)

def _gelu(x):
    return jax.nn.gelu(x, approximate=True)

def _silu(x):
    return jax.nn.silu(x)

def _sigmoid(x):
    return jax.nn.sigmoid(x)

def _layernorm(x, axis=-1, eps=1e-05):
    m = jnp.mean(x, axis=axis, keepdims=True)
    v = jnp.var(x, axis=axis, keepdims=True)
    return (x - m) / jnp.sqrt(v + eps)

def _scatter_add(tgt, idx, src, axis=0):
    return tgt.at[idx].add(src)

def _segment_sum(src, seg, n):
    return jax.ops.segment_sum(src, seg, n)
kernel_name = 'mk_xattn_ffn_d2_seqx_r8_1c0767'

def setup_inputs(seed: int=0):
    np.random.seed(seed)
    _w = jnp.asarray

    def _rec_inputs():
        import jax
        import jax.numpy as jnp
        _rk = jax.random.key(seed)
        x = -7.109e-05 + 0.9999 * jax.random.normal(jax.random.fold_in(_rk, 1), (4, 256, 256), jnp.float32)
        _lenS = 256 - jax.random.randint(jax.random.fold_in(_rk, 7), (4,), 0, max(1, 256 // 4) + 1, jnp.int32)
        _lenS2 = 256 - jax.random.randint(jax.random.fold_in(_rk, 8), (4,), 0, max(1, 256 // 4) + 1, jnp.int32)
        _ctx_512P = jax.random.normal(jax.random.fold_in(_rk, 11), (4, 16, 64), jnp.float32)
        _ctx_512c = jax.random.dirichlet(jax.random.fold_in(_rk, 511), 0.3 * jnp.ones((16,), jnp.float32), (4, 256))
        _ctx_512t = jnp.einsum('bsk,bkd->bsd', _ctx_512c, _ctx_512P)
        _ctx_512t = _ctx_512t * jax.lax.rsqrt(jnp.mean(jnp.square(_ctx_512t)) + 1e-12) * 0.953939
        ctx_512 = 2.81802e-05 + 1.00001 * (_ctx_512t + 0.3 * jax.random.normal(jax.random.fold_in(_rk, 611), (4, 256, 64), jnp.float32))
        _validS = jnp.arange(256)[None, :] < _lenS[:, None]
        _validS2 = jnp.arange(256)[None, :] < _lenS2[:, None]
        _causal = jnp.tril(jnp.ones((256, 256), dtype=bool))
        mask_SxS2_bk1 = jnp.broadcast_to(_validS2[0:1, :], (256, 256))
        mask_BxS2_bf0 = jnp.logical_not(jnp.ones((4, 256), dtype=bool))
        return (x, ctx_512, mask_SxS2_bk1, mask_BxS2_bf0)
    x, ctx_512, mask_SxS2_bk1, mask_BxS2_bf0 = _rec_inputs()

    def _L0_xattn_setup():
        import jax, jax.numpy as jnp
        import numpy as np
        EPS = 1e-06
        IMAGE_DIMS = 256
        key = jax.random.key(seed)
        k1, k2, k3 = jax.random.split(key, 3)
        B, I, J, D = (16, 256, 256, 64)
        p = jax.random.normal(k1, (B, I, J), dtype=jnp.float32)
        k_v = jax.random.normal(k2, (B, J, D), dtype=jnp.float32)
        W_k = jax.random.normal(k3, (D, D), dtype=jnp.float32) * (1.0 / np.sqrt(D))
        b_k = jnp.zeros((D,), dtype=jnp.float32)
        ln_gamma = jnp.ones((J,), dtype=jnp.float32)
        ln_beta = jnp.zeros((J,), dtype=jnp.float32)
        return {'p': p, 'k_v': k_v, 'W_k': W_k, 'b_k': b_k, 'ln_gamma': ln_gamma, 'ln_beta': ln_beta}
    _L0_xattn_all = _L0_xattn_setup()
    _L0_xattn_in = {k: v for k, v in _L0_xattn_all.items() if k in ('W_k', 'b_k', 'ln_gamma', 'ln_beta')}
    del _L0_xattn_all

    def _L0_ffn_setup():
        import jax, jax.numpy as jnp
        import numpy as np
        from jax import lax
        DIM = 256
        E = 8
        K = 2
        RANK = 32
        CAP_FACTOR = 1.25

        def gelu(x):
            return jax.nn.gelu(x, approximate=False)

        def _moe_forward(x, gate_w, w1, b1, w2, b2, wd, wu, sw1, sb1, sw2, sb2, swd, swu):
            B, S, D = x.shape
            T = B * S
            cap = max(1, int(T * CAP_FACTOR / E))
            xt = x.reshape(T, D)
            logits = xt @ gate_w
            probs_full = jax.nn.softmax(logits, axis=-1)
            top_p, top_i = lax.top_k(probs_full, K)
            out = jnp.zeros_like(xt)
            for k in range(K):
                e = top_i[:, k]
                w = top_p[:, k]
                onehot = jax.nn.one_hot(e, E, dtype=jnp.int32)
                pos_all = jnp.cumsum(onehot, axis=0) - 1
                pos = jnp.take_along_axis(pos_all, e[:, None], axis=1)[:, 0]
                keep = pos < cap
                pos_c = jnp.where(keep, pos, cap)
                buf = jnp.zeros((E, cap, D), x.dtype).at[e, pos_c].set(xt * keep[:, None].astype(x.dtype), mode='drop')
                h = gelu(jnp.einsum('ecd,edf->ecf', buf, w1) + b1[:, None, :])
                y = jnp.einsum('ecf,efd->ecd', h, w2) + b2[:, None, :]
                a = jnp.einsum('ecr,erd->ecd', gelu(jnp.einsum('ecd,edr->ecr', buf, wd)), wu)
                y = y + a
                tok = y[e, jnp.minimum(pos_c, cap - 1)]
                out = out + tok * keep[:, None].astype(x.dtype) * w[:, None]
            sh = gelu(xt @ sw1 + sb1) @ sw2 + sb2
            sh = sh + gelu(xt @ swd) @ swu
            out = out + 0.2 * sh
            return out.reshape(B, S, D)
        key = jax.random.key(seed)
        ks = jax.random.split(key, 16)
        s = 0.02
        d, h = (DIM, 4 * DIM)
        inp = {'x': jax.random.normal(ks[0], (4, 256, d), dtype=jnp.float32), 'gate_w': jax.random.normal(ks[1], (d, E), dtype=jnp.float32) * s, 'w1': jax.random.normal(ks[2], (E, d, h), dtype=jnp.float32) * s, 'b1': jnp.zeros((E, h), dtype=jnp.float32), 'w2': jax.random.normal(ks[3], (E, h, d), dtype=jnp.float32) * s, 'b2': jnp.zeros((E, d), dtype=jnp.float32), 'wd': jax.random.normal(ks[4], (E, d, RANK), dtype=jnp.float32) * s, 'wu': jax.random.normal(ks[5], (E, RANK, d), dtype=jnp.float32) * s, 'sw1': jax.random.normal(ks[6], (d, h), dtype=jnp.float32) * s, 'sb1': jnp.zeros((h,), dtype=jnp.float32), 'sw2': jax.random.normal(ks[7], (h, d), dtype=jnp.float32) * s, 'sb2': jnp.zeros((d,), dtype=jnp.float32), 'swd': jax.random.normal(ks[8], (d, RANK), dtype=jnp.float32) * s, 'swu': jax.random.normal(ks[9], (RANK, d), dtype=jnp.float32) * s}
        return inp
    _L0_ffn_all = _L0_ffn_setup()
    _L0_ffn_in = {k: v for k, v in _L0_ffn_all.items() if k in ('gate_w', 'w1', 'b1', 'w2', 'b2', 'wd', 'wu', 'sw1', 'sb1', 'sw2', 'sb2', 'swd', 'swu')}
    del _L0_ffn_all

    def _L1_xattn_setup():
        import jax, jax.numpy as jnp
        import numpy as np
        B, S, H = (8, 256, 64)
        key = jax.random.key(seed)
        kq, kk, kqc, kwq, kwk = jax.random.split(key, 5)
        q = jax.random.normal(kq, (B, S, H), dtype=jnp.float32)
        k = jax.random.normal(kk, (B, S, H), dtype=jnp.float32)
        qc_score = jax.random.uniform(kqc, (B, S, S), dtype=jnp.float32)
        attn_mask = jnp.triu(jnp.ones((S, S), dtype=bool), k=1)
        key_padding_mask = jnp.zeros((B, S), dtype=bool)
        scale = 1.0 / np.sqrt(H)
        Wq = jax.random.normal(kwq, (H, H), dtype=jnp.float32) * scale
        Wk = jax.random.normal(kwk, (H, H), dtype=jnp.float32) * scale
        bq = jnp.zeros((H,), dtype=jnp.float32)
        bk = jnp.zeros((H,), dtype=jnp.float32)
        return {'q': q, 'k': k, 'attn_mask': attn_mask, 'key_padding_mask': key_padding_mask, 'qc_score': qc_score, 'Wq': Wq, 'bq': bq, 'Wk': Wk, 'bk': bk}
    _L1_xattn_all = _L1_xattn_setup()
    _L1_xattn_in = {k: v for k, v in _L1_xattn_all.items() if k in ('Wq', 'bq', 'Wk', 'bk')}
    del _L1_xattn_all

    def _L1_ffn_setup():
        import jax, jax.numpy as jnp
        import numpy as np
        HIDDEN = 256
        INTER = 688
        LUT_SIZE = 16

        def _ghost_linear(x, idx, lut):
            w = lut[idx]
            return jnp.einsum('bsh,oh->bso', x, w)
        key = jax.random.key(seed)
        k_x, k_lut, k_g, k_u, k_d = jax.random.split(key, 5)
        x = jax.random.normal(k_x, (2, 512, HIDDEN), dtype=jnp.float32)
        lut = jax.random.normal(k_lut, (LUT_SIZE,), dtype=jnp.float32) * 0.02
        gate_idx = jax.random.randint(k_g, (INTER, HIDDEN), 0, LUT_SIZE, dtype=jnp.int32)
        up_idx = jax.random.randint(k_u, (INTER, HIDDEN), 0, LUT_SIZE, dtype=jnp.int32)
        down_idx = jax.random.randint(k_d, (HIDDEN, INTER), 0, LUT_SIZE, dtype=jnp.int32)
        return {'x': x, 'lut': lut, 'gate_idx': gate_idx, 'up_idx': up_idx, 'down_idx': down_idx}
    _L1_ffn_all = _L1_ffn_setup()
    _L1_ffn_in = {k: v for k, v in _L1_ffn_all.items() if k in ('lut', 'gate_idx', 'up_idx', 'down_idx')}
    del _L1_ffn_all
    return {'x': x, 'ctx_512': ctx_512, 'mask_SxS2_bk1': mask_SxS2_bk1, 'mask_BxS2_bf0': mask_BxS2_bf0, 'L0_xattn_W_k': _L0_xattn_in['W_k'], 'L0_xattn_b_k': _L0_xattn_in['b_k'], 'L0_xattn_ln_gamma': _L0_xattn_in['ln_gamma'], 'L0_xattn_ln_beta': _L0_xattn_in['ln_beta'], 'L0_ffn_gate_w': _L0_ffn_in['gate_w'], 'L0_ffn_w1': _L0_ffn_in['w1'], 'L0_ffn_b1': _L0_ffn_in['b1'], 'L0_ffn_w2': _L0_ffn_in['w2'], 'L0_ffn_b2': _L0_ffn_in['b2'], 'L0_ffn_wd': _L0_ffn_in['wd'], 'L0_ffn_wu': _L0_ffn_in['wu'], 'L0_ffn_sw1': _L0_ffn_in['sw1'], 'L0_ffn_sb1': _L0_ffn_in['sb1'], 'L0_ffn_sw2': _L0_ffn_in['sw2'], 'L0_ffn_sb2': _L0_ffn_in['sb2'], 'L0_ffn_swd': _L0_ffn_in['swd'], 'L0_ffn_swu': _L0_ffn_in['swu'], 'L1_xattn_Wq': _L1_xattn_in['Wq'], 'L1_xattn_bq': _L1_xattn_in['bq'], 'L1_xattn_Wk': _L1_xattn_in['Wk'], 'L1_xattn_bk': _L1_xattn_in['bk'], 'L1_ffn_lut': _L1_ffn_in['lut'], 'L1_ffn_gate_idx': _L1_ffn_in['gate_idx'], 'L1_ffn_up_idx': _L1_ffn_in['up_idx'], 'L1_ffn_down_idx': _L1_ffn_in['down_idx']}

def reference(x, ctx_512, mask_SxS2_bk1, mask_BxS2_bf0, L0_xattn_W_k, L0_xattn_b_k, L0_xattn_ln_gamma, L0_xattn_ln_beta, L0_ffn_gate_w, L0_ffn_w1, L0_ffn_b1, L0_ffn_w2, L0_ffn_b2, L0_ffn_wd, L0_ffn_wu, L0_ffn_sw1, L0_ffn_sb1, L0_ffn_sw2, L0_ffn_sb2, L0_ffn_swd, L0_ffn_swu, L1_xattn_Wq, L1_xattn_bq, L1_xattn_Wk, L1_xattn_bk, L1_ffn_lut, L1_ffn_gate_idx, L1_ffn_up_idx, L1_ffn_down_idx):
    import jax
    import jax.numpy as jnp

    def _L0_xattn_ref(p, k_v, W_k, b_k, ln_gamma, ln_beta):
        import jax, jax.numpy as jnp
        import numpy as np
        EPS = 1e-06
        IMAGE_DIMS = 256
        kv = k_v @ W_k.T + b_k
        out = jnp.einsum('bij,bjd->bid', p, kv)
        scale = IMAGE_DIMS ** (-0.5)
        sim = jnp.einsum('bid,bjd->bij', out, kv) * scale
        mu = jnp.mean(sim, axis=-1, keepdims=True)
        var = jnp.var(sim, axis=-1, keepdims=True)
        sim = (sim - mu) * jax.lax.rsqrt(var + EPS) * ln_gamma + ln_beta
        attn = jax.nn.softmax(sim, axis=-1)
        return attn

    def _L0_ffn_ref(x, gate_w, w1, b1, w2, b2, wd, wu, sw1, sb1, sw2, sb2, swd, swu):
        import jax, jax.numpy as jnp
        import numpy as np
        from jax import lax
        DIM = 256
        E = 8
        K = 2
        RANK = 32
        CAP_FACTOR = 1.25

        def gelu(x):
            return jax.nn.gelu(x, approximate=False)

        def _moe_forward(x, gate_w, w1, b1, w2, b2, wd, wu, sw1, sb1, sw2, sb2, swd, swu):
            B, S, D = x.shape
            T = B * S
            cap = max(1, int(T * CAP_FACTOR / E))
            xt = x.reshape(T, D)
            logits = xt @ gate_w
            probs_full = jax.nn.softmax(logits, axis=-1)
            top_p, top_i = lax.top_k(probs_full, K)
            out = jnp.zeros_like(xt)
            for k in range(K):
                e = top_i[:, k]
                w = top_p[:, k]
                onehot = jax.nn.one_hot(e, E, dtype=jnp.int32)
                pos_all = jnp.cumsum(onehot, axis=0) - 1
                pos = jnp.take_along_axis(pos_all, e[:, None], axis=1)[:, 0]
                keep = pos < cap
                pos_c = jnp.where(keep, pos, cap)
                buf = jnp.zeros((E, cap, D), x.dtype).at[e, pos_c].set(xt * keep[:, None].astype(x.dtype), mode='drop')
                h = gelu(jnp.einsum('ecd,edf->ecf', buf, w1) + b1[:, None, :])
                y = jnp.einsum('ecf,efd->ecd', h, w2) + b2[:, None, :]
                a = jnp.einsum('ecr,erd->ecd', gelu(jnp.einsum('ecd,edr->ecr', buf, wd)), wu)
                y = y + a
                tok = y[e, jnp.minimum(pos_c, cap - 1)]
                out = out + tok * keep[:, None].astype(x.dtype) * w[:, None]
            sh = gelu(xt @ sw1 + sb1) @ sw2 + sb2
            sh = sh + gelu(xt @ swd) @ swu
            out = out + 0.2 * sh
            return out.reshape(B, S, D)
        return _moe_forward(x, gate_w, w1, b1, w2, b2, wd, wu, sw1, sb1, sw2, sb2, swd, swu)

    def _L1_xattn_ref(q, k, attn_mask, key_padding_mask, qc_score, Wq, bq, Wk, bk):
        import jax, jax.numpy as jnp
        import numpy as np
        B, S, H = (8, 256, 64)
        qp = jnp.einsum('bsh,oh->bso', q, Wq) + bq
        kp = jnp.einsum('bth,oh->bto', k, Wk) + bk
        scaling = jnp.asarray(float(H) ** (-0.5), dtype=qp.dtype)
        scores = jnp.einsum('bsh,bth->bst', qp, kp) * scaling
        scores = scores * qc_score
        mask = attn_mask[None, :, :] | key_padding_mask[:, None, :]
        scores = jnp.where(mask, -jnp.inf, scores)
        return jax.nn.softmax(scores, axis=-1)

    def _L1_ffn_ref(x, lut, gate_idx, up_idx, down_idx):
        import jax, jax.numpy as jnp
        import numpy as np
        HIDDEN = 256
        INTER = 688
        LUT_SIZE = 16

        def _ghost_linear(x, idx, lut):
            w = lut[idx]
            return jnp.einsum('bsh,oh->bso', x, w)
        gate = _ghost_linear(x, gate_idx, lut)
        up = _ghost_linear(x, up_idx, lut)
        h = jax.nn.silu(gate) * up
        return _ghost_linear(h, down_idx, lut)
    x = x + _L0_xattn_ref(_layernorm(x, axis=-1), ctx_512, L0_xattn_W_k, L0_xattn_b_k, L0_xattn_ln_gamma, L0_xattn_ln_beta)
    x = x + _L0_ffn_ref(_layernorm(x, axis=-1), L0_ffn_gate_w, L0_ffn_w1, L0_ffn_b1, L0_ffn_w2, L0_ffn_b2, L0_ffn_wd, L0_ffn_wu, L0_ffn_sw1, L0_ffn_sb1, L0_ffn_sw2, L0_ffn_sb2, L0_ffn_swd, L0_ffn_swu)
    x = x + _L1_xattn_ref(ctx_512, ctx_512, mask_SxS2_bk1, mask_BxS2_bf0, _layernorm(x, axis=-1), L1_xattn_Wq, L1_xattn_bq, L1_xattn_Wk, L1_xattn_bk)
    x = x + _L1_ffn_ref(_layernorm(x, axis=-1), L1_ffn_lut, L1_ffn_gate_idx, L1_ffn_up_idx, L1_ffn_down_idx)
    return x

_drawn_inputs = setup_inputs


def setup_inputs(seed=0):
    import zlib

    import numpy as np

    out = dict(_drawn_inputs(seed))
    spreads = {'L0_xattn_b_k': (0.0, 2.0),
     'L0_xattn_ln_gamma': (1.0, 0.6),
     'L0_xattn_ln_beta': (0.0, 0.8),
     'L0_ffn_b1': (0.0, 0.8),
     'L0_ffn_b2': (0.0, 0.317),
     'L0_ffn_sb1': (0.0, 0.8),
     'L0_ffn_sb2': (0.0, 0.374),
     'L1_xattn_bq': (0.0, 2.0),
     'L1_xattn_bk': (0.0, 2.0)}
    factors = {'ctx_512': 2.878,
     'L0_xattn_W_k': 8.0,
     'L0_ffn_wd': 8.0,
     'L0_ffn_wu': 8.0,
     'L0_ffn_swd': 8.0,
     'L0_ffn_swu': 8.0,
     'L1_xattn_Wq': 2.961,
     'L1_xattn_Wk': 2.982}
    for name, (base, spread) in spreads.items():
        noise = np.random.default_rng([zlib.crc32(name.encode()), seed]).standard_normal(out[name].shape)
        drawn = base * np.exp(spread * noise) if base else spread * noise
        out[name] = jnp.asarray(drawn.astype(out[name].dtype))
    for name, factor in factors.items():
        out[name] = (out[name] * factor).astype(out[name].dtype)
    return out
```

```python
from contextlib import ExitStack

import concourse.bass as bass
from concourse import mybir

F32 = mybir.dt.float32
F32R = mybir.dt.float32r
BF16 = mybir.dt.bfloat16
I32 = mybir.dt.int32
U32 = mybir.dt.uint32
U8 = mybir.dt.uint8
ALU = mybir.AluOpType
ACT = mybir.ActivationFunctionType
AX = mybir.AxisListType

P = 128
B, S, D = 4, 256, 256
NTOK = B * S
T = NTOK // P
DK = D // P
H = 64
E, TOPK, RANK = 8, 2, 32
HID = 1024
CAP = int(NTOK * 1.25 / E)
SLOTS = TOPK * CAP
NF = HID // P
STEPS = NF + 1
UNITS = E + 2
UTOK = NTOK // 2
WSTEP = 512
AHEAD = 6
LAG = 2
RING = 3
INTER, LUTN = 688, 16
NG = -(-INTER // P)
LASTG = INTER - (NG - 1) * P
GATE0, UP0, DOWN0 = 0, DK * INTER, 2 * DK * INTER
LUTW = DOWN0 + NG * D
JOBS = E // 2
JW = LUTW // JOBS
JOPS = 2 * LUTN + 2
BIG = 1.0e6
LOWEST = -3.4028235e38
CONSTS = 4 + E


def program(nc, t):
    xbuf = t["xbuf"]
    ctx = ExitStack()
    with ctx:
        def sb(name, shape, dt=F32):
            return ctx.enter_context(nc.sbuf_tensor(name, shape, dt))

        def sem(name):
            return ctx.enter_context(nc.semaphore(name))

        ident = sb("ident", [P, P])
        before = sb("before", [P, P], BF16)
        ones = sb("ones", [P, P], BF16)
        expert_no = sb("expert_no", [P, E])
        minus_half = sb("minus_half", [P, 2])
        zeros = sb("zeros", [P, D])
        ctxT = sb("ctxT", [H + 1, NTOK])
        projw = sb("projw", [H + 1, 3, H])
        gamma = sb("gamma", [P, S])
        beta = sb("beta", [P, S])
        gate_w = sb("gate_w", [P, DK, E])
        gate_hi = sb("gate_hi", [P, DK, E], F32R)
        gate_lo = sb("gate_lo", [P, DK, E], F32R)
        b1 = sb("b1", [P, E + 1, NF])
        lut = sb("lut", [P, LUTN])
        x = sb("x", [P, T, D])
        xn = sb("xn", [P, T, D])
        scores = sb("scores", [P, T, S])
        mask_u8 = sb("mask_u8", [P, 2, S], U8)
        pad_u8 = sb("pad_u8", [P, B, S], U8)
        mask_add = sb("mask_add", [P, T, S], BF16)
        xT_hi = sb("xT_hi", [P, 2, DK, UTOK], F32R)
        xT_lo = sb("xT_lo", [P, 2, DK, UTOK], F32R)
        xg = sb("xg", [P, 2, 3, D])
        raw = sb("raw", [P, STEPS, WSTEP])
        w_hi = sb("w_hi", [P, STEPS, WSTEP], F32R)
        w_lo = sb("w_lo", [P, STEPS, WSTEP], F32R)
        h32 = sb("h32", [P, RING, UTOK])
        h_hi = sb("h_hi", [P, RING, UTOK], F32R)
        h_lo = sb("h_lo", [P, RING, UTOK], F32R)
        lowrank = sb("lowrank", [P, UTOK], F32R)
        ysb = sb("ysb", [P, 3, D])
        idx32 = sb("idx32", [P, JW], I32)
        idxb = sb("idxb", [P, JW], BF16)
        hit = sb("hit", [P, 2, JW], BF16)
        lacc = sb("lacc", [P, JW])
        gw_hi = sb("gw_hi", [P, LUTW], F32R)
        gw_lo = sb("gw_lo", [P, LUTW], F32R)
        gath = sb("gath", [P, 2, TOPK, D])
        outT = sb("outT", [H, 2, S])
        sm = sb("sm", [P, 2, 2, S])
        bst = sb("bst", [P, T, 6])
        mv = sb("mv", [P, 5, T, 2])
        vare = sb("vare", [P, 5, T])
        rstd = sb("rstd", [P, 5, T])
        mx = sb("mx", [P, 2, T])
        nmx = sb("nmx", [P, 2, T])
        dead = sb("dead", [P, T])
        esum = sb("esum", [P, 2, T])
        rsum = sb("rsum", [P, 2, T])
        top8 = sb("top8", [P, T, E])
        topi = sb("topi", [P, T, E], U32)
        topf = sb("topf", [P, T, TOPK])
        onehot = sb("onehot", [P, T, TOPK, E], BF16)
        ldiff = sb("ldiff", [P, T, E + TOPK])
        lexp = sb("lexp", [P, T, E + TOPK])
        lrs = sb("lrs", [P, T])
        poh = sb("poh", [P, T, TOPK, E])
        pos = sb("pos", [P, T, TOPK])
        keep = sb("keep", [P, T, TOPK])
        posc = sb("posc", [P, T, TOPK])
        base = sb("base", [P, T, TOPK])
        over = sb("over", [P, T, TOPK])
        put_f = sb("put_f", [P, T, TOPK])
        get_f = sb("get_f", [P, T, TOPK])
        put_i = sb("put_i", [P, T, TOPK], U32)
        get_i = sb("get_i", [P, T, TOPK], U32)
        wtok = sb("wtok", [P, T, TOPK])
        kvT = h32[0:H, :, :].rearrange("p a b -> p (a b)")[:, 0:NTOK]
        kv = ysb[:, :, :].rearrange("p a b -> p (a b)")[:, 0:T * H].rearrange("p (t h) -> p t h", h=H)
        qT = lacc[0:H, 0:NTOK]
        kT = gath[0:H, :, :, :].rearrange("p a b c -> p (a b c)")
        pT = xg[:, :, 0:2, :]

        hb = [ctx.enter_context(nc.psum_tensor(f"hb{i}", [P, 512], F32)) for i in range(RING)]
        yb = [ctx.enter_context(nc.psum_tensor(f"yb{i}", [P, 512], F32)) for i in range(2)]
        tb = [ctx.enter_context(nc.psum_tensor(f"tb{i}", [P, 512], F32)) for i in range(2)]
        rb = ctx.enter_context(nc.psum_tensor("rb", [P, 512], F32))
        logits = rb[:, 0:T * E].rearrange("p (t e) -> p t e", e=E)
        counts = rb[:, 128:128 + T * TOPK * E]

        x3n_ok = sem("x3n_ok")
        x_in = [sem(f"x_in{b}") for b in range(B)]
        ctx_in = sem("ctx_in")
        ln_in = sem("ln_in")
        gate_in = sem("gate_in")
        mask_in = sem("mask_in")
        lut_in = sem("lut_in")
        bias_in = sem("bias_in")
        raw_in = [sem(f"raw_in{q}") for q in range(3)]
        idx_in = sem("idx_in")
        xg_in = [sem(f"xg_in{q}") for q in range(2)]
        xbuf_zero = sem("xbuf_zero")
        scattered = sem("scattered")
        y_out = [sem(f"y_out{q}") for q in range(2)]
        gath_in = [sem(f"gath_in{q}") for q in range(2)]
        out_done = sem("out_done")
        zero_ok = sem("zero_ok")
        raw_consts = sem("raw_consts")
        consts_ok = sem("consts_ok")
        ones_row = sem("ones_row")
        bst_ok = sem("bst_ok")
        mv_ok = [sem(f"mv_ok{i}") for i in range(5)]
        vare_ok = sem("vare_ok")
        rstd_ok = [sem(f"rstd_ok{i}") for i in range(5)]
        proj_mm = sem("proj_mm")
        proj_sb = sem("proj_sb")
        p_ok = sem("p_ok")
        pT_mm = sem("pT_mm")
        pT_sb = sem("pT_sb")
        outT_mm = sem("outT_mm")
        outT_sb = sem("outT_sb")
        sim_mm = sem("sim_mm")
        sim_read = sem("sim_read")
        sm_step = sem("sm_step")
        nmx_ok = sem("nmx_ok")
        exp_ok = sem("exp_ok")
        x1_ok = sem("x1_ok")
        xn_ok = sem("xn_ok")
        qk_mm = sem("qk_mm")
        qk_sb = sem("qk_sb")
        sc_mm = sem("sc_mm")
        sc_sb = sem("sc_sb")
        mask_ok = sem("mask_ok")
        gate_ok = sem("gate_ok")
        logits_mm = sem("logits_mm")
        rt = sem("rt")
        onehot_ok = sem("onehot_ok")
        ldiff_ok = sem("ldiff_ok")
        lexp_ok = sem("lexp_ok")
        counts_mm = sem("counts_mm")
        put_ok = sem("put_ok")
        wtok_ok = sem("wtok_ok")
        xT_mm = sem("xT_mm")
        xT_hi_ok = sem("xT_hi_ok")
        xT_lo_ok = sem("xT_lo_ok")
        w_hi_ok = sem("w_hi_ok")
        w_lo_ok = sem("w_lo_ok")
        mm1 = sem("mm1")
        h32_ok = sem("h32_ok")
        h_hi_ok = sem("h_hi_ok")
        h_lo_ok = sem("h_lo_ok")
        mm2 = sem("mm2")
        y_read = sem("y_read")
        shared_read = sem("shared_read")
        lk = sem("lk")
        comb = sem("comb")
        x3T_mm = sem("x3T_mm")
        x3T_hi = sem("x3T_hi")
        x3T_lo = sem("x3T_lo")
        gu_mm = sem("gu_mm")
        silu_ok = sem("silu_ok")
        prod_ok = sem("prod_ok")
        g_hi_ok = sem("g_hi_ok")
        g_lo_ok = sem("g_lo_ok")
        down_mm = sem("down_mm")
        x4_ok = sem("x4_ok")

        block = ctx.enter_context(nc.Block())

        def third(src, q):
            return t["wpack"][src, :, q * 3 * WSTEP:(q + 1) * 3 * WSTEP].rearrange("p (s n) -> p s n", n=WSTEP)

        def blocks_of(shared):
            return UTOK // P if shared else -(-SLOTS // P)

        def columns_of(shared):
            return UTOK if shared else SLOTS

        @block.sync
        def _(sp):
            for b in range(B):
                sp.dma_start(x[:, 2 * b:2 * b + 2, :],
                             t["x"][b].rearrange("(i p) d -> p i d", p=P)).then_inc(x_in[b], 16)
                if b == 0:
                    sp.dma_start(ctxT[:, :], t["ctxT"]).then_inc(ctx_in, 16)
                    sp.dma_start(projw[:, :, :], t["projw"]).then_inc(ctx_in, 16)
            sp.dma_start(gamma[:, :], t["gamma"]).then_inc(ln_in, 16)
            sp.dma_start(beta[:, :], t["beta"]).then_inc(ln_in, 16)
            sp.dma_start(gate_w[:, :, :], t["gate_w"].rearrange("(k p) e -> p k e", p=P)).then_inc(gate_in, 16)
            for q in range(3):
                sp.dma_start(raw[:, 3 * q:3 * q + 3, :], third(0, q)).then_inc(raw_in[q], 16)
            sp.dma_start(b1[:, :, :], t["b1"]).then_inc(bias_in, 16)
            sp.wait_ge(zero_ok, 1)
            sp.dma_start(xbuf.rearrange("e (a p) d -> p (e a) d", p=SLOTS // 4),
                         zeros[0:SLOTS // 4, :].unsqueeze(1).broadcast_to([SLOTS // 4, 4 * E, D]))\
                .then_inc(xbuf_zero, 16)
            sp.dma_start(idx32[:, :], t["idx"][0]).then_inc(idx_in, 16)
            sp.dma_start(lut[:, :], t["lut"]).then_inc(lut_in, 16)
            sp.dma_start(mask_u8[:, :, :], t["mask"].rearrange("(i p) s -> p i s", p=P)).then_inc(mask_in, 16)
            sp.dma_start(pad_u8[:, :, :], t["pad"]).then_inc(mask_in, 16)

            def refill(u, src):
                for q in range(3):
                    sp.wait_ge(w_lo_ok, (u - 1) * STEPS + 3 * q + 3)
                    sp.dma_start(raw[:, 3 * q:3 * q + 3, :], third(src, q)).then_inc(raw_in[q], 16)

            def load_rows(u, turn, reused=True):
                sp.wait_ge(scattered, 16 * T * TOPK)
                if reused:
                    sp.wait_ge(xT_mm, u)
                rows = t["xbuf"][u - 1, :, :]
                sp.dma_start(xg[:, turn, 0:2, :], rows[0:2 * P, :].rearrange("(c p) d -> p c d", p=P))\
                    .then_inc(xg_in[turn], 16)
                sp.dma_start(xg[0:SLOTS - 2 * P, turn, 2, :], rows[2 * P:SLOTS, :]).then_inc(xg_in[turn], 16)

            def store_y(u):
                sp.wait_ge(y_read, u * 2)
                rows = t["ybuf"][u - 1, :, :]
                sp.dma_start(rows[0:2 * P, :].rearrange("(c p) d -> p c d", p=P), ysb[:, 0:2, :])\
                    .then_inc(y_out[0], 16)
                sp.dma_start(rows[2 * P:SLOTS, :], ysb[0:SLOTS - 2 * P, 2, :]).then_inc(y_out[1], 16)

            refill(1, 1)
            load_rows(1, 1, reused=False)
            refill(2, 2)
            load_rows(2, 0, reused=False)
            with sp.Fori(2, E - 1, 2) as u:
                sp.wait_ge(lk, u * (JOPS // 2) - JOPS + 1)
                sp.dma_start(idx32[:, :], t["idx"][u // 2, :, :]).then_inc(idx_in, 16)
                refill(u + 1, u + 1)
                load_rows(u + 1, 1)
                store_y(u - 1)
                refill(u + 2, u + 2)
                load_rows(u + 2, 0)
                store_y(u)
            refill(E + 1, 0)
            store_y(E - 1)
            store_y(E)
            for b in range(B):
                sp.wait_ge(x4_ok, b + 1)
                sp.dma_start(t["out"][b].rearrange("(i p) d -> p i d", p=P), x[:, 2 * b:2 * b + 2, :])\
                    .then_inc(out_done, 16)
            sp.wait_ge(out_done, 16 * B)

        @block.gpsimd
        def _(gp):
            gp.memset(zeros[:, :], 0.0).then_inc(zero_ok, 1)
            gp.memset(ident[:, :], 0.0).then_inc(raw_consts, 1)
            gp.memset(before[:, :], 1.0).then_inc(raw_consts, 1)
            gp.memset(ones[:, :], 1.0).then_inc(consts_ok, 1)
            gp.memset(minus_half[:, :], -0.5).then_inc(consts_ok, 1)
            for e in range(E):
                gp.memset(expert_no[:, e:e + 1], float(e)).then_inc(consts_ok, 1)
            gp.wait_ge(raw_consts, 2)
            gp.affine_select(out=ident[:, :], in_=ident[:, :], compare_op=ALU.not_equal, fill=1.0,
                             base=0, pattern=[[-1, P]], channel_multiplier=1).then_inc(consts_ok, 1)
            gp.affine_select(out=before[:, :], in_=before[:, :], compare_op=ALU.is_gt, fill=0.0,
                             base=0, pattern=[[1, P]], channel_multiplier=-1).then_inc(consts_ok, 1)
            gp.wait_ge(consts_ok, CONSTS)
            gp.memset(lowrank[H:P, :].bitcast(F32), 0.0).then_inc(ones_row, 1)
            gp.wait_ge(ones_row, 1)
            gp.memset(lowrank[H:H + 1, :].bitcast(F32), 1.0).then_inc(ones_row, 1)
            gp.wait_ge(ones_row, 2)

            done = {"vare": 0}

            def inv_std(stage, b, eps):
                ts = slice(2 * b, 2 * b + 2)
                gp.wait_ge(mv_ok[stage], 2 * b + 2)
                gp.tensor_scalar(vare[:, stage, ts], mv[:, stage, ts, 1], eps, None, ALU.add).then_inc(vare_ok, 1)
                done["vare"] += 1
                gp.wait_ge(vare_ok, done["vare"])
                gp.tensor_tensor(rstd[:, stage, ts], vare[:, stage, ts], minus_half[:, :], ALU.pow)\
                    .then_inc(rstd_ok[stage], 1)

            def split_lo(j, slot):
                gp.wait_ge(w_hi_ok, j + 1)
                gp.tensor_tensor(w_lo[:, slot, :], raw[:, slot, :], w_hi[:, slot, :].bitcast(F32), ALU.subtract)\
                    .then_inc(w_lo_ok, 1)

            for b in range(B):
                inv_std(0, b, 1e-5)
            inv_std(1, 0, S * 1e-6)
            split_lo(0, 0)
            inv_std(1, 1, S * 1e-6)
            split_lo(1, 1)
            inv_std(1, 2, S * 1e-6)
            inv_std(2, 0, 1e-5)
            inv_std(1, 3, S * 1e-6)
            inv_std(2, 1, 1e-5)
            inv_std(2, 2, 1e-5)
            inv_std(2, 3, 1e-5)
            for j in range(2, AHEAD):
                split_lo(j, j)
            gp.wait_ge(xbuf_zero, 16)
            gp.wait_ge(put_ok, 1)
            rows = t["xbuf"].rearrange("e s d -> (e s) d")
            for s in range(STEPS):
                split_lo(s + AHEAD, (s + AHEAD) % STEPS)
                for n in range(2 * s, min(2 * s + 2, T * TOPK)):
                    tile, k = n // TOPK, n % TOPK
                    gp.indirect_dma_start(rows, bass.IndirectOffsetOnAxis(ap=put_i[:, tile, k:k + 1], axis=0),
                                          xn[:, tile, :], None, bounds_check=E * SLOTS - 1, oob_is_err=False)\
                        .then_inc(scattered, 16)
            def unit(u):
                for s in range(STEPS):
                    split_lo(u * STEPS + s + AHEAD, (s + AHEAD) % STEPS)

            unit(1)
            with gp.Fori(2, E - 1, 2) as u:
                unit(u)
                unit(u + 1)
            unit(E)
            for s in range(STEPS - AHEAD):
                split_lo((E + 1) * STEPS + s + AHEAD, s + AHEAD)
            for q in range(2):
                gp.wait_ge(y_out[q], 16 * E)
            yrows = t["ybuf"].rearrange("e s d -> (e s) d")
            for b in range(B):
                for tile in (2 * b, 2 * b + 1):
                    if tile >= 2:
                        gp.wait_ge(comb, 2 * (tile - 1))
                    for k in range(TOPK):
                        gp.indirect_dma_start(gath[:, tile % 2, k, :], None, yrows,
                                              bass.IndirectOffsetOnAxis(ap=get_i[:, tile, k:k + 1], axis=0))\
                            .then_inc(gath_in[tile % 2], 16)
                if b == 1:
                    inv_std(3, 0, 1e-5)
                    inv_std(3, 1, 1e-5)
                    inv_std(4, 0, 1e-5)
                    inv_std(4, 1, 1e-5)
                if b >= 2:
                    inv_std(3, b, 1e-5)
                    inv_std(4, b, 1e-5)

        @block.tensor
        def _(pe):
            pe.wait_ge(ctx_in, 32)
            for n in range(2):
                pe.matmul(hb[n][0:H, :], projw[:, 0, :], ctxT[:, n * 512:(n + 1) * 512], start=True, stop=True)\
                    .then_inc(proj_mm, 1)
            for j in range(T):
                mm = pe.matmul(rb[:, j * H:(j + 1) * H], ctxT[:, j * P:(j + 1) * P], projw[:, 0, :],
                               start=True, stop=True)
            mm.then_inc(proj_mm, 1)
            pe.wait_ge(consts_ok, CONSTS)

            def transpose_p(b):
                pe.wait_ge(p_ok, 2 * b + 2)
                if b >= 2:
                    pe.wait_ge(pT_sb, b - 1)
                for i in range(2):
                    for k in range(2):
                        mm = pe.transpose(tb[b % 2][:, k * S + i * P:k * S + (i + 1) * P],
                                          xn[:, 2 * b + i, k * P:(k + 1) * P], ident[:, :])
                mm.then_inc(pT_mm, 1)

            def mix(b):
                pe.wait_ge(pT_sb, b + 1)
                pe.wait_ge(proj_sb, 3)
                if b >= 2:
                    pe.wait_ge(outT_sb, b - 1)
                for k in range(2):
                    mm = pe.matmul(yb[b % 2][0:H, 0:S], kv[:, 2 * b + k, :], pT[:, b % 2, k, :],
                                   start=(k == 0), stop=(k == 1))
                mm.then_inc(outT_mm, 1)
                pe.wait_ge(outT_sb, b + 1)
                if b == RING:
                    pe.wait_ge(sim_read, 2)
                for i in range(2):
                    mm = pe.matmul(hb[b % RING][:, i * S:(i + 1) * S], outT[:, b % 2, i * P:(i + 1) * P],
                                   kvT[:, b * S:(b + 1) * S], start=True, stop=True)
                mm.then_inc(sim_mm, 1)

            transpose_p(0)
            transpose_p(1)
            mix(0)
            transpose_p(2)
            mix(1)
            transpose_p(3)
            mix(2)
            mix(3)
            pe.wait_ge(pT_sb, B)
            pe.wait_ge(outT_sb, B)
            for w, bank in ((1, tb), (2, yb)):
                for n in range(2):
                    pe.matmul(bank[n][0:H, :], projw[:, w, :], ctxT[:, n * 512:(n + 1) * 512],
                              start=True, stop=True).then_inc(qk_mm, 1)
            for b in range(B):
                pe.wait_ge(qk_sb, 4)
                if b >= 2:
                    pe.wait_ge(sc_sb, b - 1)
                for i in range(2):
                    mm = pe.matmul(tb[b % 2][:, i * S:(i + 1) * S], qT[:, (2 * b + i) * P:(2 * b + i + 1) * P],
                                   kT[:, b * S:(b + 1) * S], start=True, stop=True)
                mm.then_inc(sc_mm, 1)

            def transpose_rows(rows, blocks, width):
                for k in range(DK):
                    for c in range(blocks):
                        n = min(P, width - c * P)
                        mm = pe.transpose(tb[k][:, c * P:c * P + n], rows(c)[0:n, k * P:(k + 1) * P],
                                          ident[0:n, 0:n])
                mm.then_inc(xT_mm, 1)

            pe.wait_ge(sc_sb, B)
            pe.wait_ge(gate_ok, 2)
            for half in range(2):
                pe.wait_ge(xn_ok, 4 * half + 4)
                if half:
                    pe.wait_ge(xT_lo_ok, 1)
                transpose_rows(lambda c: xn[:, 4 * half + c, :], 4, UTOK)
                pe.wait_ge(xT_lo_ok, half + 1)
                for c in range(4):
                    terms = [(a, w, k) for k in range(DK) for a in (xT_hi, xT_lo) for w in (gate_hi, gate_lo)]
                    for n, (a, w, k) in enumerate(terms):
                        mm = pe.matmul(logits[:, 4 * half + c, :], a[:, half, k, c * P:(c + 1) * P], w[:, k, :],
                                       start=(n == 0), stop=(n == len(terms) - 1))
                mm.then_inc(logits_mm, 1)

            def first(g, u, s, shared, turn):
                pe.wait_ge(w_lo_ok, g + 1)
                if not isinstance(g, int) or g >= RING:
                    pe.wait_ge(h_hi_ok, g - RING + 1)
                n = columns_of(shared)
                terms = [(w, a, k) for k in range(DK) for w, a in ((w_hi, xT_hi), (w_lo, xT_hi), (w_hi, xT_lo))]
                for i, (w, a, k) in enumerate(terms):
                    mm = pe.matmul(hb[s % RING][:, 0:n], w[:, s, k * P:(k + 1) * P], a[:, turn, k, 0:n],
                                   start=(i == 0), stop=(i == len(terms) - 1))
                mm.then_inc(mm1, 1)

            def second(g, s, shared):
                pe.wait_ge(h_lo_ok, g + 1)
                for c in range(blocks_of(shared)):
                    if s < NF:
                        terms = [(h_hi, w_hi), (h_lo, w_hi), (h_hi, w_lo)]
                        terms = [(h[:, s % RING, c * P:(c + 1) * P], w) for h, w in terms]
                    else:
                        terms = [(lowrank[:, c * P:(c + 1) * P], w) for w in (w_hi, w_lo)]
                    for i, (h, w) in enumerate(terms):
                        mm = pe.matmul(yb[c // 2][:, (c % 2) * D:(c % 2 + 1) * D], h, w[:, s, 2 * P:WSTEP],
                                       start=(s == 0 and i == 0 and c % 2 == 0),
                                       stop=(s == STEPS - 1 and i == len(terms) - 1), skip_group_check=True)
                mm.then_inc(mm2, 1)

            def unit(u, turn, shared=False, after_shared=False, rows=None):
                pe.wait_ge(xT_lo_ok, u + 2 if not shared or u else 1)
                for s in range(STEPS):
                    g = u * STEPS + s
                    first(g, u, s, shared, turn)
                    if s >= LAG:
                        if s == LAG and after_shared:
                            pe.wait_ge(shared_read, 2)
                        elif s == LAG and (not isinstance(u, int) or u > 0):
                            pe.wait_ge(y_read, u * 2 - 2)
                        second(g - LAG, s - LAG, shared)
                    elif not isinstance(u, int) or u > 0:
                        second(g - LAG, STEPS + s - LAG, after_shared)
                    if rows is not None and s == 5:
                        rows(u + 1, 1 - turn)
                    if shared and u == 0 and s == 1:
                        pe.wait_ge(onehot_ok, 1)
                        oh = onehot[:, :, :, :].rearrange("p t k e -> p (t k e)")
                        w = TOPK * E
                        pe.matmul(counts, before[:, :], oh, start=True, stop=False, skip_group_check=True)
                        for j in range(T - 1):
                            later = T - 1 - j
                            src = onehot[:, j, :, :].rearrange("p k e -> p (k e)").unsqueeze(1)
                            mm = pe.matmul(counts[:, (j + 1) * w:], ones[:, :],
                                           src.broadcast_to([P, later, w]),
                                           start=False, stop=(j == T - 2), skip_group_check=True)
                        mm.then_inc(counts_mm, 1)

            def expert_rows(u, turn):
                pe.wait_ge(xT_lo_ok, u + 1)
                if isinstance(u, int):
                    pe.wait_ge(xg_in[turn], 32 * ((u + 1) // 2))
                else:
                    pe.wait_ge(xg_in[turn], (u + turn) * 16)
                transpose_rows(lambda c: xg[:, turn, c, :], 3, SLOTS)

            def shared_rows(u, turn):
                pe.wait_ge(xT_lo_ok, u + 1)
                transpose_rows(lambda c: xn[:, 4 + c, :], 4, UTOK)

            pe.wait_ge(ones_row, 2)
            unit(0, 0, shared=True)
            expert_rows(1, 1)
            unit(1, 1, after_shared=True, rows=expert_rows)
            with pe.Fori(2, E - 1, 2) as u:
                unit(u, 0, rows=expert_rows)
                unit(u + 1, 1, rows=expert_rows)
            unit(E, 0, rows=shared_rows)
            unit(E + 1, 1, shared=True)
            for s in range(STEPS - LAG, STEPS):
                second((E + 1) * STEPS + s, s, True)

            def transpose_x3(b):
                pe.wait_ge(x3n_ok, 2 * b + 2)
                if b < 2:
                    pe.wait_ge(xT_lo_ok, E + 3)
                else:
                    pe.wait_ge(x3T_lo, b - 1)
                for i in range(2):
                    for k in range(DK):
                        mm = pe.transpose(tb[b % 2][:, k * S + i * P:k * S + (i + 1) * P],
                                          xn[:, 2 * b + i, k * P:(k + 1) * P], ident[:, :])
                mm.then_inc(x3T_mm, 1)

            def gate_up(b, f):
                n = b * NG + f
                if n < RING:
                    pe.wait_ge(h_hi_ok, UNITS * STEPS)
                else:
                    pe.wait_ge(prod_ok, n - RING + 1)
                if f == 0:
                    pe.wait_ge(x3T_lo, b + 1)
                for part, first_col in enumerate((GATE0, UP0)):
                    terms = [(w, a, k) for k in range(DK)
                             for w, a in ((gw_hi, xT_hi), (gw_lo, xT_hi), (gw_hi, xT_lo))]
                    for i, (w, a, k) in enumerate(terms):
                        at = first_col + k * INTER + f * P
                        mm = pe.matmul(hb[n % RING][:, part * S:(part + 1) * S], w[:, at:at + P],
                                       a[:, b % 2, k, 0:S], start=(i == 0), stop=(i == len(terms) - 1))
                mm.then_inc(gu_mm, 1)

            def down(b, f):
                n = b * NG + f
                if n == 0:
                    pe.wait_ge(shared_read, 4)
                if f == 0 and b >= 2:
                    pe.wait_ge(x4_ok, b - 1)
                pe.wait_ge(g_lo_ok, n + 1)
                K = P if f < NG - 1 else LASTG
                for i in range(2):
                    for j, (h, w) in enumerate(((h_hi, gw_hi), (h_lo, gw_hi), (h_hi, gw_lo))):
                        at = DOWN0 + f * D
                        mm = pe.matmul(yb[b % 2][:, i * D:(i + 1) * D], h[0:K, n % RING, i * P:(i + 1) * P],
                                       w[0:K, at:at + D], start=(f == 0 and i == 0 and j == 0),
                                       stop=(f == NG - 1 and j == 2), skip_group_check=True)
                mm.then_inc(down_mm, 1)

            pe.wait_ge(lk, JOBS * JOPS)
            transpose_x3(0)
            for n in range(B * NG + LAG):
                if n < B * NG:
                    gate_up(n // NG, n % NG)
                if n >= LAG:
                    down((n - LAG) // NG, (n - LAG) % NG)
                if n % NG == 3 and n // NG + 1 < B:
                    transpose_x3(n // NG + 1)

        @block.scalar
        def _(act):
            def copy(dst, src, scale=1.0):
                return act.activation(dst, src, ACT.Copy, scale=scale)

            act.wait_ge(proj_mm, 3)
            for n in range(2):
                copy(kvT[:, n * 512:(n + 1) * 512], hb[n][0:H, :]).then_inc(proj_sb, 1)
            copy(kv, rb[:, :].rearrange("p (t h) -> p t h", h=H)).then_inc(proj_sb, 1)
            act.wait_ge(gate_in, 16)
            copy(gate_hi[:, :, :], gate_w[:, :, :]).then_inc(gate_ok, 1)

            def pT_copy(b):
                act.wait_ge(pT_mm, b + 1)
                if b >= 2:
                    act.wait_ge(outT_mm, b - 1)
                copy(pT[:, b % 2, :, :], tb[b % 2][:, :].rearrange("p (k s) -> p k s", k=2)).then_inc(pT_sb, 1)

            def outT_copy(b):
                act.wait_ge(outT_mm, b + 1)
                if b >= 2:
                    act.wait_ge(sim_mm, b - 1)
                copy(outT[:, b % 2, :], yb[b % 2][0:H, 0:S]).then_inc(outT_sb, 1)

            def exps(which, b):
                for i in range(2):
                    tile = 2 * b + i
                    act.wait_ge(nmx_ok, 2 * (which * B + b) + i + 1)
                    act.activation(sm[:, b % 2, i, :], sm[:, b % 2, i, :], ACT.Exp, bias=nmx[:, which, tile:tile + 1],
                                   accum_out=esum[:, which, tile:tile + 1]).then_inc(exp_ok, 1)

            def split_hi(j, slot, u):
                act.wait_ge(raw_in[slot // 3], u * 16 + 16)
                if not isinstance(j, int) or j >= STEPS:
                    act.wait_ge(mm2, j - STEPS + 1)
                copy(w_hi[:, slot, :], raw[:, slot, :]).then_inc(w_hi_ok, 1)

            pT_copy(0)
            pT_copy(1)
            outT_copy(0)
            pT_copy(2)
            outT_copy(1)
            pT_copy(3)
            split_hi(0, 0, 0)
            outT_copy(2)
            exps(0, 0)
            outT_copy(3)
            split_hi(1, 1, 0)
            exps(0, 1)
            for n in range(4):
                act.wait_ge(qk_mm, n + 1)
                copy((qT if n < 2 else kT)[:, (n % 2) * 512:(n % 2 + 1) * 512], (tb if n < 2 else yb)[n % 2][0:H, :])\
                    .then_inc(qk_sb, 1)
            exps(0, 2)
            for b in range(B):
                act.wait_ge(sc_mm, b + 1)
                copy(scores[:, 2 * b:2 * b + 2, :], tb[b % 2][:, :].rearrange("p (i s) -> p i s", i=2),
                     scale=float(H) ** -0.5).then_inc(sc_sb, 1)
                if b == 1:
                    exps(0, 3)
            for j in range(2, AHEAD):
                split_hi(j, j, 0)

            def rows_hi(count, turn, width):
                act.wait_ge(xT_mm, count)
                for k in range(DK):
                    copy(xT_hi[:, turn, k, 0:width], tb[k][:, 0:width]).then_inc(xT_hi_ok, 1)

            rows_hi(1, 0, UTOK)
            rows_hi(2, 1, UTOK)
            act.wait_ge(ldiff_ok, 1)
            act.activation(lexp[:, :, :], ldiff[:, :, :], ACT.Exp).then_inc(lexp_ok, 1)
            act.wait_ge(bias_in, 16)

            def gelu(g, s, n, expert):
                act.wait_ge(mm1, g + 1)
                if not isinstance(g, int) or g >= RING:
                    act.wait_ge(h_lo_ok, g - RING + 1)
                    act.wait_ge(mm2, g - RING + 1)
                if s < NF:
                    bias = b1[:, expert, s:s + 1]
                    act.activation(h32[:, s % RING, 0:n], hb[s % RING][:, 0:n], ACT.Gelu, bias=bias).then_inc(h32_ok, 1)
                    act.activation(h_hi[:, s % RING, 0:n], hb[s % RING][:, 0:n], ACT.Gelu, bias=bias)\
                        .then_inc(h_hi_ok, 1)
                else:
                    act.activation(h32[0:H, s % RING, 0:n], hb[s % RING][0:H, 0:n], ACT.Gelu).then_inc(h32_ok, 1)
                    act.activation(lowrank[0:H, 0:n], hb[s % RING][0:H, 0:n], ACT.Gelu).then_inc(h_hi_ok, 1)

            def read_y(u, g):
                act.wait_ge(mm2, g)
                if not isinstance(u, int) or u > 1:
                    act.wait_ge(y_out[0], u * 16 - 16)
                copy(ysb[:, 0:2, :], yb[0][:, :].rearrange("p (c d) -> p c d", c=2)).then_inc(y_read, 1)
                if not isinstance(u, int) or u > 1:
                    act.wait_ge(y_out[1], u * 16 - 16)
                copy(ysb[0:SLOTS - 2 * P, 2, :], yb[1][0:SLOTS - 2 * P, 0:D]).then_inc(y_read, 1)

            def unit(u, turn, shared=False, after_shared=False, width=0):
                for s in range(STEPS):
                    g = u * STEPS + s
                    gelu(g, s, columns_of(shared), 0 if shared else u)
                    if not isinstance(u, int) or u <= E or s + AHEAD < STEPS:
                        split_hi(g + AHEAD, (s + AHEAD) % STEPS, u + (s + AHEAD) // STEPS)
                    if s == 1 and not after_shared and (not isinstance(u, int) or u > 0):
                        read_y(u - 1, u * STEPS)
                    if s == 6 and width:
                        rows_hi(u + 3, 1 - turn, width)
                    if u_is(u, E + 1) and s == 6:
                        exps(1, 0)
                        exps(1, 1)

            def u_is(u, n):
                return isinstance(u, int) and u == n

            unit(0, 0, shared=True)
            rows_hi(3, 1, SLOTS)
            unit(1, 1, after_shared=True, width=SLOTS)
            with act.Fori(2, E - 1, 2) as u:
                unit(u, 0, width=SLOTS)
                unit(u + 1, 1, width=SLOTS)
            unit(E, 0, width=UTOK)
            unit(E + 1, 1, shared=True)
            def x3T_copy(b):
                act.wait_ge(x3T_mm, b + 1)
                if b >= 2:
                    act.wait_ge(gu_mm, (b - 1) * NG)
                copy(xT_hi[:, b % 2, :, 0:S], tb[b % 2][:, :].rearrange("p (k s) -> p k s", k=DK)).then_inc(x3T_hi, 1)

            x3T_copy(0)
            for n in range(B * NG):
                b, f = n // NG, n % NG
                if f == 0 and b < 2:
                    exps(1, b + 2)
                act.wait_ge(gu_mm, n + 1)
                if n >= RING:
                    act.wait_ge(g_lo_ok, n - RING + 1)
                act.activation(h32[:, n % RING, S:2 * S], hb[n % RING][:, 0:S], ACT.Silu).then_inc(silu_ok, 1)
                act.wait_ge(prod_ok, n + 1)
                if n >= RING:
                    act.wait_ge(down_mm, n - RING + 1)
                copy(h_hi[:, n % RING, 0:S], h32[:, n % RING, 0:S]).then_inc(g_hi_ok, 1)
                if f == 4 and b + 1 < B:
                    x3T_copy(b + 1)

        @block.vector
        def _(dve):
            n_bst = {"n": 0}
            n_sm = {"n": 0}

            def stats(stage, tile, src):
                dve.bn_stats(bst[:, tile, :], src).then_inc(bst_ok, 1)
                n_bst["n"] += 1
                dve.wait_ge(bst_ok, n_bst["n"])
                dve.bn_aggr(mv[:, stage, tile, :], bst[:, tile, :]).then_inc(mv_ok[stage], 1)

            def normalise(stage, tile, dst, src, done):
                dve.tensor_scalar(dst, src, mv[:, stage, tile, 0:1], rstd[:, stage, tile:tile + 1],
                                  ALU.subtract, ALU.mult).then_inc(done, 1)

            def own(ins):
                ins.then_inc(sm_step, 1)
                n_sm["n"] += 1
                dve.wait_ge(sm_step, n_sm["n"])

            for b in range(B):
                dve.wait_ge(x_in[b], 16)
                for tile in (2 * b, 2 * b + 1):
                    stats(0, tile, x[:, tile, :])
            for b in range(B):
                dve.wait_ge(rstd_ok[0], b + 1)
                for tile in (2 * b, 2 * b + 1):
                    normalise(0, tile, xn[:, tile, :], x[:, tile, :], p_ok)
            dve.wait_ge(gate_ok, 1)
            dve.tensor_tensor(gate_lo[:, :, :], gate_w[:, :, :], gate_hi[:, :, :].bitcast(F32), ALU.subtract)\
                .then_inc(gate_ok, 1)
            dve.wait_ge(ln_in, 32)

            def sim_stats(b):
                dve.wait_ge(sim_mm, b + 1)
                for i in range(2):
                    stats(1, 2 * b + i, hb[b % RING][:, i * S:(i + 1) * S])

            def maxima(which, b, extra):
                for i in range(2):
                    tile = 2 * b + i
                    row = sm[:, b % 2, i, :]
                    own(dve.tensor_tensor_reduce(row, row, extra(i), 1.0, LOWEST, ALU.add, ALU.max,
                                                 mx[:, which, tile:tile + 1]))
                    dve.tensor_scalar(nmx[:, which, tile:tile + 1], mx[:, which, tile:tile + 1], -1.0,
                                      dead[:, tile:tile + 1] if which else 0.0, ALU.mult, ALU.add).then_inc(nmx_ok, 1)

            def sim_rows(b):
                dve.wait_ge(rstd_ok[1], b + 1)
                if b >= 2:
                    dve.wait_ge(exp_ok, 2 * b - 2)
                for i in range(2):
                    normalise(1, 2 * b + i, sm[:, b % 2, i, :], hb[b % RING][:, i * S:(i + 1) * S], sim_read)
                dve.wait_ge(sim_read, 2 * b + 2)
                both = sm[:, b % 2, :, :]
                own(dve.tensor_tensor(both, both, gamma[:, :].unsqueeze(1).broadcast_to([P, 2, S]), ALU.mult))
                maxima(0, b, lambda i: beta[:, :])

            def add_probs(which, b, stage):
                ts = slice(2 * b, 2 * b + 2)
                dve.wait_ge(exp_ok, 2 * (which * B + b) + 2)
                own(dve.reciprocal(rsum[:, which, ts], esum[:, which, ts]))
                for i in range(2):
                    tile = 2 * b + i
                    own(dve.scalar_tensor_tensor(out=x[:, tile, :], in0=sm[:, b % 2, i, :],
                                                 scalar=rsum[:, which, tile:tile + 1], in1=x[:, tile, :],
                                                 op0=ALU.mult, op1=ALU.add))
                    stats(stage, tile, x[:, tile, :])

            def norm_x(stage, b, done):
                dve.wait_ge(rstd_ok[stage], b + 1)
                for tile in (2 * b, 2 * b + 1):
                    normalise(stage, tile, xn[:, tile, :], x[:, tile, :], done)

            sim_stats(0)
            sim_stats(1)
            sim_rows(0)
            sim_rows(1)
            sim_stats(2)
            add_probs(0, 0, 2)
            sim_rows(2)
            sim_stats(3)
            add_probs(0, 1, 2)
            norm_x(2, 0, xn_ok)
            sim_rows(3)
            add_probs(0, 2, 2)
            norm_x(2, 1, xn_ok)
            add_probs(0, 3, 2)
            norm_x(2, 2, xn_ok)
            norm_x(2, 3, xn_ok)

            def rows_lo(count, turn, width):
                for k in range(DK):
                    dve.wait_ge(xT_hi_ok, (count - 1) * DK + k + 1)
                    ins = dve.tensor_tensor(xT_lo[:, turn, k, 0:width], tb[k][:, 0:width],
                                            xT_hi[:, turn, k, 0:width].bitcast(F32), ALU.subtract)
                ins.then_inc(xT_lo_ok, 1)

            rows_lo(1, 0, UTOK)
            rows_lo(2, 1, UTOK)

            n_rt = {"n": 0}

            def rts(ins):
                ins.then_inc(rt, 1)
                n_rt["n"] += 1

            def rt_wait():
                dve.wait_ge(rt, n_rt["n"])

            dve.wait_ge(logits_mm, 2)
            dve.wait_ge(consts_ok, CONSTS)
            for tile in range(T):
                rts(dve.max(top8[:, tile, :], logits[:, tile, :]))
            rt_wait()
            for tile in range(T):
                rts(dve.max_index(topi[:, tile, :], top8[:, tile, :], logits[:, tile, :]))
            rts(dve.tensor_tensor(ldiff[:, :, 0:E], logits, top8[:, :, 0:1].broadcast_to([P, T, E]), ALU.subtract))
            dve.tensor_tensor(ldiff[:, :, E:E + TOPK], top8[:, :, 0:TOPK],
                              top8[:, :, 0:1].broadcast_to([P, T, TOPK]), ALU.subtract).then_inc(ldiff_ok, 1)
            rt_wait()
            rts(dve.tensor_copy(topf[:, :, :], topi[:, :, 0:TOPK]))
            rt_wait()
            shape = [P, T, TOPK, E]
            dve.tensor_tensor(onehot[:, :, :, :], topf[:, :, :].unsqueeze(3).broadcast_to(shape),
                              expert_no[:, :].unsqueeze(1).unsqueeze(1).broadcast_to(shape), ALU.is_equal)\
                .then_inc(onehot_ok, 1)
            for k in range(TOPK):
                rts(dve.tensor_scalar(base[:, :, k:k + 1], topf[:, :, k:k + 1], float(SLOTS), float(k * CAP),
                                      ALU.mult, ALU.add))
            dve.wait_ge(lexp_ok, 1)
            rts(dve.tensor_reduce(lrs[:, :], lexp[:, :, 0:E], AX.X, ALU.add))
            rt_wait()
            rts(dve.reciprocal(lrs[:, :], lrs[:, :]))
            dve.wait_ge(counts_mm, 1)
            dve.wait_ge(onehot_ok, 1)
            rts(dve.tensor_tensor(poh[:, :, :, :], onehot[:, :, :, :],
                                  counts.rearrange("p (t k e) -> p t k e", t=T, k=TOPK), ALU.mult))
            rt_wait()
            rts(dve.tensor_reduce(pos[:, :, :], poh[:, :, :, :], AX.X, ALU.add))
            rt_wait()
            rts(dve.tensor_scalar(over[:, :, :], pos[:, :, :], float(CAP), BIG, ALU.is_ge, ALU.mult))
            rts(dve.tensor_tensor(put_f[:, :, :], pos[:, :, :], base[:, :, :], ALU.add))
            rt_wait()
            rts(dve.tensor_tensor(put_f[:, :, :], put_f[:, :, :], over[:, :, :], ALU.add))
            rt_wait()
            dve.tensor_copy(put_i[:, :, :], put_f[:, :, :]).then_inc(put_ok, 1)
            rts(dve.tensor_scalar(keep[:, :, :], pos[:, :, :], float(CAP), None, ALU.is_lt))
            rts(dve.tensor_scalar(posc[:, :, :], pos[:, :, :], float(CAP - 1), None, ALU.min))
            rt_wait()
            rts(dve.tensor_tensor(get_f[:, :, :], posc[:, :, :], base[:, :, :], ALU.add))
            rts(dve.tensor_tensor(wtok[:, :, :], lexp[:, :, E:E + TOPK], keep[:, :, :], ALU.mult))
            rt_wait()
            dve.tensor_copy(get_i[:, :, :], get_f[:, :, :]).then_inc(wtok_ok, 1)
            dve.tensor_tensor(wtok[:, :, :], wtok[:, :, :], lrs[:, :].unsqueeze(2).broadcast_to([P, T, TOPK]),
                              ALU.mult).then_inc(wtok_ok, 1)
            dve.wait_ge(mask_in, 32)
            for b in range(B):
                own(dve.tensor_tensor(mask_add[:, 2 * b:2 * b + 2, :], mask_u8[:, :, :],
                                      pad_u8[:, b, :].unsqueeze(1).broadcast_to([P, 2, S]), ALU.max))
            own(dve.tensor_reduce(dead[:, :], mask_add[:, :, :], AX.X, ALU.min))
            own(dve.tensor_scalar(dead[:, :], dead[:, :], 3.0e38, 1.0e10, ALU.mult, ALU.mult))
            own(dve.tensor_tensor(dead[:, :], dead[:, :], dead[:, :], ALU.subtract))
            own(dve.tensor_scalar(mask_add[:, :, :], mask_add[:, :, :], -3.0e38, None, ALU.mult))

            def lo(g, s, n):
                dve.wait_ge(h32_ok, g + 1)
                dve.wait_ge(h_hi_ok, g + 1)
                r = s % RING
                if s < NF:
                    dve.tensor_tensor(h_lo[:, r, 0:n], h32[:, r, 0:n], h_hi[:, r, 0:n].bitcast(F32), ALU.subtract)\
                        .then_inc(h_lo_ok, 1)
                else:
                    dve.tensor_tensor(lowrank[RANK:H, 0:n], h32[RANK:H, r, 0:n], lowrank[RANK:H, 0:n].bitcast(F32),
                                      ALU.subtract).then_inc(h_lo_ok, 1)

            def lookup(n, before_job, loads, at):
                if n == 0:
                    dve.wait_ge(idx_in, loads)
                    dve.wait_ge(lut_in, 16)
                    dve.tensor_copy(idxb[:, :], idx32[:, :]).then_inc(lk, 1)
                    dve.wait_ge(lk, before_job + 1)
                    dve.tensor_scalar(lacc[:, :], idxb[:, :], 0.0, lut[:, 0:1], ALU.is_equal, ALU.mult).then_inc(lk, 1)
                elif n < LUTN:
                    dve.tensor_scalar(hit[:, n % 2, :], idxb[:, :], float(n), None, ALU.is_equal).then_inc(lk, 1)
                    dve.wait_ge(lk, before_job + 2 * n + 1)
                    dve.scalar_tensor_tensor(out=lacc[:, :], in0=hit[:, n % 2, :], scalar=lut[:, n:n + 1],
                                             in1=lacc[:, :], op0=ALU.mult, op1=ALU.add).then_inc(lk, 1)
                elif n == LUTN:
                    dve.wait_ge(lk, before_job + 2 * LUTN)
                    dve.tensor_copy(gw_hi[:, at], lacc[:, :]).then_inc(lk, 1)
                else:
                    dve.wait_ge(lk, before_job + 2 * LUTN + 1)
                    dve.tensor_tensor(gw_lo[:, at], lacc[:, :], gw_hi[:, at].bitcast(F32), ALU.subtract)\
                        .then_inc(lk, 1)

            def unit(u, turn, shared=False, after_shared=False, width=0, job=None, extra=None):
                for s in range(STEPS):
                    lo(u * STEPS + s, s, columns_of(shared))
                    if s == 1 and after_shared:
                        add_shared(0)
                    if s == 6 and width:
                        rows_lo(u + 3, 1 - turn, width)
                    if job is not None:
                        lookup(s + job[0], *job[1:])
                    if extra is not None:
                        extra(s)

            def add_shared(half):
                dve.wait_ge(mm2, STEPS if half == 0 else UNITS * STEPS)
                for i in range(2):
                    ts = slice(4 * half + 2 * i, 4 * half + 2 * i + 2)
                    dve.scalar_tensor_tensor(out=x[:, ts, :], in0=yb[i][:, :].rearrange("p (c d) -> p c d", c=2),
                                             scalar=0.2, in1=x[:, ts, :], op0=ALU.mult, op1=ALU.add)\
                        .then_inc(shared_read, 1)

            def add_experts(tile):
                dve.wait_ge(gath_in[tile % 2], 32 * (tile // 2 + 1))
                for k in range(TOPK):
                    dve.scalar_tensor_tensor(out=x[:, tile, :], in0=gath[:, tile % 2, k, :],
                                             scalar=wtok[:, tile, k:k + 1], in1=x[:, tile, :],
                                             op0=ALU.mult, op1=ALU.add).then_inc(comb, 1)
                    dve.wait_ge(comb, 2 * tile + k + 1)

            def attend(b):
                dve.wait_ge(rstd_ok[3], b + 1)
                if b >= 2:
                    dve.wait_ge(exp_ok, 2 * (B + b) - 2)
                for i in range(2):
                    own(dve.tensor_scalar(sm[:, b % 2, i, :], x[:, 2 * b + i, :], mv[:, 3, 2 * b + i, 0:1],
                                          rstd[:, 3, 2 * b + i:2 * b + i + 1], ALU.subtract, ALU.mult))
                both = sm[:, b % 2, :, :]
                own(dve.tensor_tensor(both, both, scores[:, 2 * b:2 * b + 2, :], ALU.mult))
                maxima(1, b, lambda i: mask_add[:, 2 * b + i, :])

            def combine(b):
                for tile in (2 * b, 2 * b + 1):
                    add_experts(tile)
                    stats(3, tile, x[:, tile, :])

            def tail(s):
                if s == 4:
                    combine(0)
                if s == 5:
                    combine(1)
                if s == 6:
                    attend(0)
                    attend(1)
                if s == 7:
                    add_probs(1, 0, 4)
                    add_probs(1, 1, 4)
                if s == 8:
                    norm_x(4, 0, x3n_ok)
                    norm_x(4, 1, x3n_ok)

            unit(0, 0, shared=True, job=(0, 0, 16, slice(0, JW)))
            dve.wait_ge(wtok_ok, 2)
            rows_lo(3, 1, SLOTS)
            unit(1, 1, after_shared=True, width=SLOTS, job=(STEPS, 0, 16, slice(0, JW)))
            with dve.Fori(2, E - 1, 2) as u:
                at = bass.ds(u * (JW // 2), JW)
                unit(u, 0, width=SLOTS, job=(0, u * (JOPS // 2), u * 8 + 16, at))
                unit(u + 1, 1, width=SLOTS, job=(STEPS, u * (JOPS // 2), u * 8 + 16, at))
            unit(E, 0, width=UTOK)
            dve.wait_ge(shared_read, 2)
            unit(E + 1, 1, shared=True, extra=tail)
            add_shared(1)
            dve.wait_ge(shared_read, 4)

            def x3T_split(b):
                dve.wait_ge(x3T_hi, b + 1)
                dve.tensor_tensor(xT_lo[:, b % 2, :, 0:S], tb[b % 2][:, :].rearrange("p (k s) -> p k s", k=DK),
                                  xT_hi[:, b % 2, :, 0:S].bitcast(F32), ALU.subtract).then_inc(x3T_lo, 1)

            def finish(b):
                dve.wait_ge(down_mm, (b + 1) * NG)
                ts = slice(2 * b, 2 * b + 2)
                dve.tensor_tensor(x[:, ts, :], x[:, ts, :], yb[b % 2][:, :].rearrange("p (c d) -> p c d", c=2),
                                  ALU.add).then_inc(x4_ok, 1)

            x3T_split(0)
            for n in range(B * NG):
                b, f = n // NG, n % NG
                if f == 0 and b < 2:
                    combine(b + 2)
                    attend(b + 2)
                dve.wait_ge(silu_ok, n + 1)
                r = n % RING
                dve.tensor_tensor(h32[:, r, 0:S], h32[:, r, S:2 * S], hb[r][:, S:2 * S], ALU.mult).then_inc(prod_ok, 1)
                dve.wait_ge(g_hi_ok, n + 1)
                dve.tensor_tensor(h_lo[:, r, 0:S], h32[:, r, 0:S], h_hi[:, r, 0:S].bitcast(F32), ALU.subtract)\
                    .then_inc(g_lo_ok, 1)
                if f == 0 and b < 2:
                    add_probs(1, b + 2, 4)
                if f == 1 and b < 2:
                    norm_x(4, b + 2, x3n_ok)
                if f == 2 and b > 0:
                    finish(b - 1)
                if f == 4 and b + 1 < B:
                    x3T_split(b + 1)
            finish(B - 1)


def kernel(**inputs):
    import numpy as np
    import concourse.bacc as bacc
    from concourse.bass_utils import run_bass_kernel_spmd

    def arr(name):
        return np.ascontiguousarray(inputs[name])

    def lanes(a, n=P):
        return np.ascontiguousarray(np.broadcast_to(a, (n, *a.shape)))

    def stream(w1, w2, wd, wu, b2):
        first = w1.reshape(DK, P, NF, P).transpose(1, 2, 0, 3).reshape(P, NF, DK * P)
        second = w2.reshape(NF, P, D).transpose(1, 0, 2)
        low = np.concatenate([wd] * (P // RANK), axis=1).reshape(DK, P, P).transpose(1, 0, 2).reshape(P, 1, DK * P)
        up = np.concatenate([wu, wu, b2[None, :], np.zeros((P - 2 * RANK - 1, D), w1.dtype)])[:, None, :]
        main = np.concatenate([first, second], axis=2)
        return np.concatenate([main, np.concatenate([low, up], axis=2)], axis=1).reshape(P, STEPS * WSTEP)

    ffn = {n: arr("L0_ffn_" + n) for n in
           ("w1", "b1", "w2", "b2", "wd", "wu", "sw1", "sb1", "sw2", "sb2", "swd", "swu", "gate_w")}
    wpack = np.stack([stream(ffn["sw1"], ffn["sw2"], ffn["swd"], ffn["swu"], ffn["sb2"])]
                     + [stream(*(ffn[n][e] for n in ("w1", "w2", "wd", "wu", "b2"))) for e in range(E)])
    b1 = np.concatenate([ffn["sb1"][None, :], ffn["b1"]]).reshape(E + 1, NF, P).transpose(2, 0, 1)
    one = np.ones((1, NTOK), np.float32)
    ctxT = np.concatenate([arr("ctx_512").reshape(NTOK, H).T, one])
    projw = np.stack([np.concatenate([arr(w).T, arr(b)[None, :]]) for w, b in
                      (("L0_xattn_W_k", "L0_xattn_b_k"), ("L1_xattn_Wq", "L1_xattn_bq"), ("L1_xattn_Wk", "L1_xattn_bk"))],
                     axis=1)
    gate, up, down = (arr("L1_ffn_" + n + "_idx") for n in ("gate", "up", "down"))
    down_t = np.concatenate([down.T, np.zeros((NG * P - INTER, D), down.dtype)])
    idx = np.concatenate([a.T.reshape(DK, P, INTER).transpose(1, 0, 2).reshape(P, DK * INTER) for a in (gate, up)]
                         + [down_t.reshape(NG, P, D).transpose(1, 0, 2).reshape(P, NG * D)], axis=1)
    arrays = {
        "x": arr("x"), "ctxT": ctxT, "projw": projw,
        "gamma": lanes(arr("L0_xattn_ln_gamma")), "beta": lanes(arr("L0_xattn_ln_beta")),
        "gate_w": ffn["gate_w"], "b1": b1, "wpack": wpack,
        "idx": idx.reshape(P, JOBS, JW).transpose(1, 0, 2), "lut": lanes(arr("L1_ffn_lut")),
        "mask": arr("mask_SxS2_bk1"), "pad": lanes(arr("mask_BxS2_bf0")),
    }
    arrays = {n + "_dram": np.ascontiguousarray(a) for n, a in arrays.items()}
    nc = bacc.Bacc("TRN2", target_bir_lowering=False, num_devices=1)
    tensors = {n[:-5]: nc.dram_tensor(n, a.shape, mybir.dt.from_np(a.dtype), kind="ExternalInput").ap()
               for n, a in arrays.items()}
    tensors["xbuf"] = nc.dram_tensor("xbuf_dram", (E, SLOTS, D), F32).ap()
    tensors["ybuf"] = nc.dram_tensor("ybuf_dram", (E, SLOTS, D), F32).ap()
    tensors["out"] = nc.dram_tensor("out_dram", (B, S, D), F32, kind="ExternalOutput").ap()
    program(nc, tensors)
    return run_bass_kernel_spmd(nc, [arrays], core_ids=[0]).results[0]["out_dram"]
```

```python
from contextlib import ExitStack

import concourse.bass as bass
from concourse import mybir

F32 = mybir.dt.float32
F32R = mybir.dt.float32r
BF16 = mybir.dt.bfloat16
I32 = mybir.dt.int32
U32 = mybir.dt.uint32
U8 = mybir.dt.uint8
ALU = mybir.AluOpType
ACT = mybir.ActivationFunctionType
AX = mybir.AxisListType

P = 128
B, S, D = 4, 256, 256
NTOK = B * S
T = NTOK // P
DK = D // P
H = 64
E, TOPK, RANK = 8, 2, 32
HID = 1024
CAP = int(NTOK * 1.25 / E)
SLOTS = TOPK * CAP
NF = HID // P
STEPS = NF + 1
UNITS = E + 2
UTOK = NTOK // 2
WSTEP = 512
AHEAD = 6
LAG = 2
RING = 3
INTER, LUTN = 688, 16
NG = -(-INTER // P)
LASTG = INTER - (NG - 1) * P
GATE0, UP0, DOWN0 = 0, DK * INTER, 2 * DK * INTER
LUTW = DOWN0 + NG * D
JOB_W = (1216, 832, 832, 832, LUTW - 1216 - 3 * 832)
JOB_AT = tuple(sum(JOB_W[:n]) for n in range(5))
JOBS, JW = len(JOB_W), max(JOB_W)
LOOP_AT = JOB_AT[1] - JOB_W[1]
EARLY = 4
JOPS = 2 * LUTN + 2
BIG = 1.0e6
LOWEST = -3.4028235e38
CONSTS = 8 + E
ROW = D + TOPK


def program(nc, t):
    xbuf = t["xbuf"]
    ctx = ExitStack()
    with ctx:
        def sb(name, shape, dt=F32):
            return ctx.enter_context(nc.sbuf_tensor(name, shape, dt))

        def sem(name):
            return ctx.enter_context(nc.semaphore(name))

        ident = sb("ident", [P, P])
        before = sb("before", [P, P], BF16)
        ones = sb("ones", [P, P], BF16)
        expert_no = sb("expert_no", [P, E])
        minus_half = sb("minus_half", [P, 2])
        zeros = sb("zeros", [P, ROW])
        round_of = sb("round_of", [P, 3, TOPK])
        ctxT = sb("ctxT", [H + 1, NTOK])
        projw = sb("projw", [H + 1, 3, H])
        gamma = sb("gamma", [P, S])
        beta = sb("beta", [P, S])
        gate_w = sb("gate_w", [P, DK, E])
        gate_parts = sb("gate_parts", [P, DK, P], F32R)
        logitsT = sb("logitsT", [2 * E, NTOK])
        logits = sb("logits", [P, T, E])
        b1 = sb("b1", [P, E + 1, NF])
        lut = sb("lut", [P, LUTN])
        x = sb("x", [P, T, D])
        xn = sb("xn", [P, T, ROW])
        scores = sb("scores", [P, T, S])
        mask_u8 = sb("mask_u8", [P, 2, S], U8)
        pad_u8 = sb("pad_u8", [P, B, S], U8)
        mask_add = sb("mask_add", [P, T, S], BF16)
        xT_hi = sb("xT_hi", [P, 2, DK, UTOK], F32R)
        xT_lo = sb("xT_lo", [P, 2, DK, UTOK], F32R)
        xg = sb("xg", [P, 2, 3, ROW])
        wrow = sb("wrow", [P, 3, TOPK])
        wsel = sb("wsel", [P, 2, 3])
        raw = sb("raw", [P, STEPS, WSTEP])
        w_hi = sb("w_hi", [P, STEPS, WSTEP], F32R)
        w_lo = sb("w_lo", [P, STEPS, WSTEP], F32R)
        h32 = sb("h32", [P, RING, UTOK])
        h_hi = sb("h_hi", [P, RING, UTOK], F32R)
        h_lo = sb("h_lo", [P, RING, UTOK], F32R)
        lowrank = sb("lowrank", [P, UTOK], F32R)
        ysb = sb("ysb", [P, 3, D])
        idx32 = sb("idx32", [P, JW], I32)
        idxb = sb("idxb", [P, JW], BF16)
        hit = sb("hit", [P, 2, JW], BF16)
        lacc = sb("lacc", [P, JW])
        gw_hi = sb("gw_hi", [P, LUTW], F32R)
        gw_lo = sb("gw_lo", [P, LUTW], F32R)
        kT = sb("kT", [H, NTOK])
        outT = sb("outT", [H, 2, S])
        sm = sb("sm", [P, 2, 2, S])
        bst = sb("bst", [P, T, 6])
        mv = sb("mv", [P, 5, T, 2])
        vare = sb("vare", [P, 5, T])
        rstd = sb("rstd", [P, 5, T])
        mx = sb("mx", [P, 2, T])
        nmx = sb("nmx", [P, 2, T])
        nmr = sb("nmr", [P, T])
        dead = sb("dead", [P, T])
        esum = sb("esum", [P, 2, T])
        rsum = sb("rsum", [P, 2, T])
        top8 = sb("top8", [P, T, E])
        topi = sb("topi", [P, T, E], U32)
        topf = sb("topf", [P, T, TOPK])
        onehot = sb("onehot", [P, T, TOPK, E], BF16)
        ldiff = sb("ldiff", [P, T, E + TOPK])
        lexp = sb("lexp", [P, T, E + TOPK])
        lrs = sb("lrs", [P, T])
        poh = sb("poh", [P, T, TOPK, E])
        pos = sb("pos", [P, T, TOPK])
        base = sb("base", [P, T, TOPK])
        over = sb("over", [P, T, TOPK])
        put_f = sb("put_f", [P, T, TOPK])
        get_f = sb("get_f", [P, T, TOPK])
        put_i = sb("put_i", [P, T, TOPK], U32)
        get_i = sb("get_i", [P, T, TOPK], U32)
        kvT = h32[0:H, :, :].rearrange("p a b -> p (a b)")[:, 0:NTOK]
        kv = ysb[:, :, :].rearrange("p a b -> p (a b)")[:, 0:T * H].rearrange("p (t h) -> p t h", h=H)
        pT = xg[:, :, 0:2, 0:S]
        qT = xg[0:H, :, 0:2, 0:S]

        hb = [ctx.enter_context(nc.psum_tensor(f"hb{i}", [P, 512], F32)) for i in range(RING)]
        yb = [ctx.enter_context(nc.psum_tensor(f"yb{i}", [P, 512], F32)) for i in range(2)]
        tb = [ctx.enter_context(nc.psum_tensor(f"tb{i}", [P, 512], F32)) for i in range(2)]
        rb = ctx.enter_context(nc.psum_tensor("rb", [P, 512], F32))
        down_banks = (rb, yb[0])
        parts = rb[:, 0:T * 2 * E].rearrange("p (t a e) -> p t a e", a=2, e=E)
        counts = rb[:, 128:128 + T * TOPK * E]

        x3n_ok = sem("x3n_ok")
        x_in = [sem(f"x_in{b}") for b in range(B)]
        ctx_in = sem("ctx_in")
        ln_in = sem("ln_in")
        gate_in = sem("gate_in")
        mask_in = sem("mask_in")
        lut_in = sem("lut_in")
        bias_in = sem("bias_in")
        raw_in = [sem(f"raw_in{q}") for q in range(3)]
        idx_in = sem("idx_in")
        xg_in = [sem(f"xg_in{q}") for q in range(2)]
        xbuf_zero = sem("xbuf_zero")
        scattered = sem("scattered")
        y_out = [sem(f"y_out{q}") for q in range(2)]
        gath_in = [sem(f"gath_in{j}") for j in range(T)]
        out_done = sem("out_done")
        zero_ok = sem("zero_ok")
        raw_consts = sem("raw_consts")
        consts_ok = sem("consts_ok")
        ones_row = sem("ones_row")
        bst_ok = sem("bst_ok")
        mv_ok = [sem(f"mv_ok{i}") for i in range(5)]
        vare_ok = sem("vare_ok")
        rstd_ok = [sem(f"rstd_ok{i}") for i in range(5)]
        proj_mm = sem("proj_mm")
        proj_sb = sem("proj_sb")
        p_ok = sem("p_ok")
        pT_mm = sem("pT_mm")
        pT_sb = sem("pT_sb")
        outT_mm = sem("outT_mm")
        outT_sb = sem("outT_sb")
        sim_mm = sem("sim_mm")
        sm_step = sem("sm_step")
        nmx_ok = sem("nmx_ok")
        exp_ok = sem("exp_ok")
        xn_ok = sem("xn_ok")
        qk_mm = sem("qk_mm")
        qk_sb = sem("qk_sb")
        sc_mm = sem("sc_mm")
        sc_sb = sem("sc_sb")
        mask_ok = sem("mask_ok")
        gate_ok = sem("gate_ok")
        logitsT_mm = sem("logitsT_mm")
        logitsT_sb = sem("logitsT_sb")
        logits_mm = sem("logits_mm")
        rt = sem("rt")
        onehot_ok = sem("onehot_ok")
        ldiff_ok = sem("ldiff_ok")
        lexp_ok = sem("lexp_ok")
        counts_mm = sem("counts_mm")
        put_ok = sem("put_ok")
        wtok_ok = sem("wtok_ok")
        get_ok = sem("get_ok")
        wsel_ok = sem("wsel_ok")
        wr_ok = sem("wr_ok")
        xT_mm = sem("xT_mm")
        xT_hi_ok = sem("xT_hi_ok")
        xT_lo_ok = sem("xT_lo_ok")
        w_hi_ok = sem("w_hi_ok")
        w_lo_ok = sem("w_lo_ok")
        mm1 = sem("mm1")
        h32_ok = sem("h32_ok")
        h_hi_ok = sem("h_hi_ok")
        h_lo_ok = sem("h_lo_ok")
        mm2 = sem("mm2")
        y_read = sem("y_read")
        shared_read = sem("shared_read")
        lk = sem("lk")
        nmr_ok = sem("nmr_ok")
        sm_in = sem("sm_in")
        gain_ok = sem("gain_ok")
        x3T_mm = sem("x3T_mm")
        x3T_hi = sem("x3T_hi")
        x3T_lo = sem("x3T_lo")
        gu_mm = sem("gu_mm")
        silu_ok = sem("silu_ok")
        prod_ok = sem("prod_ok")
        g_lo_ok = sem("g_lo_ok")
        down_mm = sem("down_mm")
        x4_ok = sem("x4_ok")

        block = ctx.enter_context(nc.Block())

        def third(src, q):
            return t["wpack"][src, :, q * 3 * WSTEP:(q + 1) * 3 * WSTEP].rearrange("p (s n) -> p s n", n=WSTEP)

        def blocks_of(shared):
            return UTOK // P if shared else -(-SLOTS // P)

        def u_is(u, n):
            return isinstance(u, int) and u == n

        def exp_rows(which, b):
            return sm[:, b % 2, :, :] if which == 0 or b < 2 else xg[:, b - 2, 0:2, 0:S]

        def columns_of(shared):
            return UTOK if shared else SLOTS

        @block.sync
        def _(sp):
            for b in range(B):
                sp.dma_start(x[:, 2 * b:2 * b + 2, :],
                             t["x"][b].rearrange("(i p) d -> p i d", p=P)).then_inc(x_in[b], 16)
                if b == 0:
                    sp.dma_start(ctxT[:, :], t["ctxT"]).then_inc(ctx_in, 16)
                    sp.dma_start(projw[:, :, :], t["projw"]).then_inc(ctx_in, 16)
            sp.dma_start(gamma[:, :], t["gamma"]).then_inc(ln_in, 16)
            sp.dma_start(beta[:, :], t["beta"]).then_inc(ln_in, 16)
            sp.dma_start(gate_w[:, :, :], t["gate_w"].rearrange("(k p) e -> p k e", p=P)).then_inc(gate_in, 16)
            for q in range(3):
                sp.dma_start(raw[:, 3 * q:3 * q + 3, :], third(0, q)).then_inc(raw_in[q], 16)
                if q == 0:
                    sp.dma_start(idx32[:, 0:JOB_W[0]], t["idx"][:, 0:JOB_W[0]]).then_inc(idx_in, 16)
                    sp.dma_start(lut[:, :], t["lut"]).then_inc(lut_in, 16)
            sp.dma_start(b1[:, :, :], t["b1"]).then_inc(bias_in, 16)
            sp.wait_ge(zero_ok, 1)
            sp.dma_start(xbuf.rearrange("e (a p) d -> p (e a) d", p=SLOTS // 4),
                         zeros[0:SLOTS // 4, :].unsqueeze(1).broadcast_to([SLOTS // 4, 4 * E, ROW]))\
                .then_inc(xbuf_zero, 16)
            sp.dma_start(t["ybuf"][E * SLOTS:E * SLOTS + 1, :], zeros[0:1, 0:D]).then_inc(xbuf_zero, 16)
            sp.dma_start(mask_u8[:, :, :], t["mask"].rearrange("(i p) s -> p i s", p=P)).then_inc(mask_in, 16)
            sp.dma_start(pad_u8[:, :, :], t["pad"]).then_inc(mask_in, 16)

            def refill(u, src):
                for q in range(3):
                    sp.wait_ge(w_lo_ok, (u - 1) * STEPS + 3 * q + 3)
                    sp.dma_start(raw[:, 3 * q:3 * q + 3, :], third(src, q)).then_inc(raw_in[q], 16)

            def load_rows(u, turn, reused=True):
                rows = t["xbuf"][u - 1, :, :]
                sp.wait_ge(scattered, 16 * T * TOPK)
                if reused:
                    sp.wait_ge(wsel_ok, u - 2)
                sp.dma_start(xg[:, turn, 0:2, :], rows[0:2 * P, :].rearrange("(c p) d -> p c d", p=P))\
                    .then_inc(xg_in[turn], 16)
                sp.dma_start(xg[0:SLOTS - 2 * P, turn, 2, :], rows[2 * P:SLOTS, :]).then_inc(xg_in[turn], 16)

            yrows3 = t["ybuf"][0:E * SLOTS, :].rearrange("(e s) d -> e s d", s=SLOTS)

            def store_y(u):
                sp.wait_ge(y_read, u * 3)
                rows = yrows3[u - 1, :, :]
                sp.dma_start(rows[0:2 * P, :].rearrange("(c p) d -> p c d", p=P), ysb[:, 0:2, :])\
                    .then_inc(y_out[0], 16)
                sp.dma_start(rows[2 * P:SLOTS, :], ysb[0:SLOTS - 2 * P, 2, :]).then_inc(y_out[1], 16)

            refill(1, 1)
            load_rows(1, 1, reused=False)
            load_rows(2, 0, reused=False)
            refill(2, 2)
            with sp.Fori(2, E - 1, 2) as u:
                sp.wait_ge(lk, u * (JOPS // 2) - JOPS + 1)
                sp.dma_start(idx32[:, 0:JOB_W[1]], t["idx"][:, bass.ds(u * (JOB_W[1] // 2) + LOOP_AT, JOB_W[1])])\
                    .then_inc(idx_in, 16)
                load_rows(u + 1, 1)
                refill(u + 1, u + 1)
                store_y(u - 1)
                load_rows(u + 2, 0)
                refill(u + 2, u + 2)
                store_y(u)
            sp.wait_ge(lk, 3 * JOPS + 1)
            sp.dma_start(idx32[:, 0:JOB_W[4]], t["idx"][:, JOB_AT[4]:LUTW]).then_inc(idx_in, 16)
            refill(E + 1, 0)
            store_y(E - 1)
            store_y(E)
            for b in range(B):
                sp.wait_ge(x4_ok, b + 1)
                sp.dma_start(t["out"][b].rearrange("(i p) d -> p i d", p=P), x[:, 2 * b:2 * b + 2, :])\
                    .then_inc(out_done, 16)
            sp.wait_ge(out_done, 16 * B)

        @block.gpsimd
        def _(gp):
            gp.memset(zeros[:, :], 0.0).then_inc(zero_ok, 1)
            gp.memset(ident[:, :], 0.0).then_inc(raw_consts, 1)
            gp.memset(before[:, :], 1.0).then_inc(raw_consts, 1)
            gp.memset(ones[:, :], 1.0).then_inc(consts_ok, 1)
            gp.memset(minus_half[:, :], -0.5).then_inc(consts_ok, 1)
            gp.memset(xg[:, :, 2, :], 0.0).then_inc(consts_ok, 1)
            gp.memset(round_of[:, 0, 0:1], 1.0).then_inc(raw_consts, 1)
            gp.memset(round_of[:, 0, 1:2], 0.0).then_inc(raw_consts, 1)
            gp.memset(round_of[:, 1:3, 0:1], 0.0).then_inc(raw_consts, 1)
            gp.memset(round_of[:, 1:3, 1:2], 1.0).then_inc(raw_consts, 1)
            for e in range(E):
                gp.memset(expert_no[:, e:e + 1], float(e)).then_inc(consts_ok, 1)
            gp.wait_ge(raw_consts, 6)
            gp.memset(round_of[0:CAP - P, 1, 0:1], 1.0).then_inc(consts_ok, 1)
            gp.memset(round_of[0:CAP - P, 1, 1:2], 0.0).then_inc(consts_ok, 1)
            gp.memset(gate_parts[:, :, :].bitcast(F32), 0.0).then_inc(consts_ok, 1)
            gp.affine_select(out=ident[:, :], in_=ident[:, :], compare_op=ALU.not_equal, fill=1.0,
                             base=0, pattern=[[-1, P]], channel_multiplier=1).then_inc(consts_ok, 1)
            gp.affine_select(out=before[:, :], in_=before[:, :], compare_op=ALU.is_gt, fill=0.0,
                             base=0, pattern=[[1, P]], channel_multiplier=-1).then_inc(consts_ok, 1)
            gp.wait_ge(consts_ok, CONSTS)
            gp.memset(lowrank[H:P, :].bitcast(F32), 0.0).then_inc(ones_row, 1)
            gp.wait_ge(ones_row, 1)
            gp.memset(lowrank[H:H + 1, :].bitcast(F32), 1.0).then_inc(ones_row, 1)
            gp.wait_ge(ones_row, 2)

            done = {"vare": 0}

            def inv_std(stage, b, eps):
                ts = slice(2 * b, 2 * b + 2)
                gp.wait_ge(mv_ok[stage], 2 * b + 2)
                gp.tensor_scalar(vare[:, stage, ts], mv[:, stage, ts, 1], eps, None, ALU.add).then_inc(vare_ok, 1)
                done["vare"] += 1
                gp.wait_ge(vare_ok, done["vare"])
                gp.tensor_tensor(rstd[:, stage, ts], vare[:, stage, ts], minus_half[:, :], ALU.pow)\
                    .then_inc(rstd_ok[stage], 1)

            def split_lo(j, slot):
                gp.wait_ge(w_hi_ok, j + 1)
                gp.tensor_tensor(w_lo[:, slot, :], raw[:, slot, :], w_hi[:, slot, :].bitcast(F32), ALU.subtract)\
                    .then_inc(w_lo_ok, 1)

            def gain(b):
                gp.wait_ge(sm_in, 2 * b + 2)
                both = sm[:, b % 2, :, :]
                gp.tensor_tensor(both, both, gamma[:, :].unsqueeze(1).broadcast_to([P, 2, S]), ALU.mult)\
                    .then_inc(gain_ok, 1)

            for b in range(B):
                inv_std(0, b, 1e-5)
            gp.wait_ge(ln_in, 32)
            for j in range(3):
                split_lo(j, j)
            inv_std(1, 0, S * 1e-6)
            split_lo(3, 3)
            gain(0)
            inv_std(1, 1, S * 1e-6)
            split_lo(4, 4)
            gain(1)
            inv_std(1, 2, S * 1e-6)
            inv_std(2, 0, 1e-5)
            gain(2)
            inv_std(1, 3, S * 1e-6)
            inv_std(2, 1, 1e-5)
            gain(3)
            split_lo(5, 5)
            inv_std(2, 2, 1e-5)
            inv_std(2, 3, 1e-5)
            for j in range(6, STEPS):
                split_lo(j, j)
            gp.wait_ge(xbuf_zero, 32)
            gp.wait_ge(put_ok, 1)
            gp.wait_ge(wtok_ok, 1)
            rows = t["xbuf"].rearrange("e s d -> (e s) d")
            for tile in range(T):
                for k in range(TOPK):
                    gp.indirect_dma_start(rows, bass.IndirectOffsetOnAxis(ap=put_i[:, tile, k:k + 1], axis=0),
                                          xn[:, tile, :], None, bounds_check=E * SLOTS - 1, oob_is_err=False)\
                        .then_inc(scattered, 16)
            gp.wait_ge(w_lo_ok, STEPS + AHEAD)

            def unit(u):
                for s in range(STEPS):
                    split_lo(u * STEPS + s + AHEAD, (s + AHEAD) % STEPS)

            unit(1)
            with gp.Fori(2, E - 1, 2) as u:
                unit(u)
                unit(u + 1)
            unit(E)
            for s in range(STEPS - AHEAD):
                split_lo((E + 1) * STEPS + s + AHEAD, s + AHEAD)
            gp.wait_ge(get_ok, 1)
            gp.wait_ge(shared_read, 2)
            for q in range(2):
                gp.wait_ge(y_out[q], 16 * E)

            def get(tile, k):
                if k:
                    gp.wait_ge(gath_in[tile], 16)
                gp.indirect_dma_start(x[:, tile, :], None, t["ybuf"],
                                      bass.IndirectOffsetOnAxis(ap=get_i[:, tile, k:k + 1], axis=0),
                                      compute_op=ALU.add).then_inc(gath_in[tile], 16)

            for tile, k in ((0, 0), (1, 0), (2, 0), (0, 1), (1, 1), (3, 0), (2, 1), (3, 1)):
                get(tile, k)
            inv_std(3, 0, 1e-5)
            for tile, k in ((4, 0), (5, 0), (6, 0)):
                get(tile, k)
            inv_std(3, 1, 1e-5)
            get(4, 1)
            inv_std(4, 0, 1e-5)
            for tile, k in ((5, 1), (7, 0), (6, 1), (7, 1)):
                get(tile, k)
            for n in range(B * NG):
                gp.wait_ge(prod_ok, n + 1)
                r = n % RING
                gp.tensor_tensor(h_lo[:, r, 0:S], h32[:, r, 0:S], h_hi[:, r, 0:S].bitcast(F32), ALU.subtract)\
                    .then_inc(g_lo_ok, 1)
                if n == 1:
                    inv_std(4, 1, 1e-5)
                elif n == 3:
                    inv_std(3, 2, 1e-5)
                elif n == 4:
                    inv_std(3, 3, 1e-5)
                elif n == 8:
                    inv_std(4, 2, 1e-5)
                elif n == 12:
                    inv_std(4, 3, 1e-5)

        @block.tensor
        def _(pe):
            pe.wait_ge(ctx_in, 32)
            for n in range(2):
                pe.matmul(hb[n][0:H, :], projw[:, 0, :], ctxT[:, n * 512:(n + 1) * 512], start=True, stop=True)\
                    .then_inc(proj_mm, 1)
            for j in range(T):
                mm = pe.matmul(rb[:, j * H:(j + 1) * H], ctxT[:, j * P:(j + 1) * P], projw[:, 0, :],
                               start=True, stop=True)
            mm.then_inc(proj_mm, 1)
            pe.wait_ge(consts_ok, CONSTS)

            def transpose_p(b):
                pe.wait_ge(p_ok, 2 * b + 2)
                if b >= 2:
                    pe.wait_ge(pT_sb, b - 1)
                for i in range(2):
                    for k in range(2):
                        mm = pe.transpose(tb[b % 2][:, k * S + i * P:k * S + (i + 1) * P],
                                          xn[:, 2 * b + i, k * P:(k + 1) * P], ident[:, :])
                mm.then_inc(pT_mm, 1)

            def mix(b):
                pe.wait_ge(pT_sb, b + 1)
                pe.wait_ge(proj_sb, 3)
                if b >= 2:
                    pe.wait_ge(outT_sb, b - 1)
                for k in range(2):
                    mm = pe.matmul(yb[b % 2][0:H, 0:S], kv[:, 2 * b + k, :], pT[:, b % 2, k, :],
                                   start=(k == 0), stop=(k == 1))
                mm.then_inc(outT_mm, 1)
                pe.wait_ge(outT_sb, b + 1)
                if b == RING:
                    pe.wait_ge(sm_in, 2)
                for i in range(2):
                    mm = pe.matmul(hb[b % RING][:, i * S:(i + 1) * S], outT[:, b % 2, i * P:(i + 1) * P],
                                   kvT[:, b * S:(b + 1) * S], start=True, stop=True)
                mm.then_inc(sim_mm, 1)

            transpose_p(0)
            transpose_p(1)
            mix(0)
            transpose_p(2)
            mix(1)
            transpose_p(3)
            mix(2)
            mix(3)
            pe.wait_ge(pT_sb, B)
            pe.wait_ge(outT_sb, B)
            for w, bank in ((1, tb), (2, yb)):
                for n in range(2):
                    pe.matmul(bank[n][0:H, :], projw[:, w, :], ctxT[:, n * 512:(n + 1) * 512],
                              start=True, stop=True).then_inc(qk_mm, 1)
            for b in range(B):
                pe.wait_ge(qk_sb, 4)
                if b >= 2:
                    pe.wait_ge(sc_sb, b - 1)
                for i in range(2):
                    mm = pe.matmul(tb[b % 2][:, i * S:(i + 1) * S], qT[:, b // 2, b % 2, i * P:(i + 1) * P],
                                   kT[:, b * S:(b + 1) * S], start=True, stop=True)
                mm.then_inc(sc_mm, 1)

            def transpose_rows(rows, blocks, width):
                for k in range(DK):
                    for c in range(blocks):
                        n = min(P, width - c * P)
                        mm = pe.transpose(tb[k][:, c * P:c * P + n], rows(c)[0:n, k * P:(k + 1) * P],
                                          ident[0:n, 0:n])
                mm.then_inc(xT_mm, 1)

            pe.wait_ge(sc_sb, B)
            pe.wait_ge(gate_ok, 2)
            for half in range(2):
                pe.wait_ge(xn_ok, 4 * half + 4)
                if half:
                    pe.wait_ge(xT_lo_ok, 1)
                transpose_rows(lambda c: xn[:, 4 * half + c, :], 4, UTOK)
                pe.wait_ge(xT_lo_ok, half + 1)
                if half:
                    pe.wait_ge(logitsT_sb, 1)
                for n in range(2 * DK):
                    k, a = n % DK, (xT_hi, xT_lo)[n // DK]
                    mm = pe.matmul(rb[:, :], gate_parts[:, k, :], a[:, half, k, :], start=(n == 0), stop=(n == 3))
                mm.then_inc(logitsT_mm, 1)
            pe.wait_ge(logitsT_sb, 2)
            for j in range(T):
                mm = pe.transpose(rb[:, j * 2 * E:(j + 1) * 2 * E], logitsT[:, j * P:(j + 1) * P],
                                  ident[0:2 * E, 0:2 * E])
            mm.then_inc(logits_mm, 1)

            def first(g, u, s, shared, turn):
                pe.wait_ge(w_lo_ok, g + 1)
                if not isinstance(g, int) or g >= RING:
                    pe.wait_ge(h_hi_ok, g - RING + 1)
                n = columns_of(shared)
                terms = [(w, a, k) for k in range(DK) for w, a in ((w_hi, xT_hi), (w_lo, xT_hi), (w_hi, xT_lo))]
                for i, (w, a, k) in enumerate(terms):
                    mm = pe.matmul(hb[s % RING][:, 0:n], w[:, s, k * P:(k + 1) * P], a[:, turn, k, 0:n],
                                   start=(i == 0), stop=(i == len(terms) - 1))
                mm.then_inc(mm1, 1)

            def second(g, s, shared):
                pe.wait_ge(h_lo_ok, g + 1)
                for c in range(blocks_of(shared)):
                    if s < NF:
                        terms = [(h_hi, w_hi), (h_lo, w_hi), (h_hi, w_lo)]
                        terms = [(h[:, s % RING, c * P:(c + 1) * P], w) for h, w in terms]
                    else:
                        terms = [(lowrank[:, c * P:(c + 1) * P], w) for w in (w_hi, w_lo)]
                    for i, (h, w) in enumerate(terms):
                        mm = pe.matmul(yb[c // 2][:, (c % 2) * D:(c % 2 + 1) * D], h, w[:, s, 2 * P:WSTEP],
                                       start=(s == 0 and i == 0 and c % 2 == 0),
                                       stop=(s == STEPS - 1 and i == len(terms) - 1), skip_group_check=True)
                mm.then_inc(mm2, 1)

            def unit(u, turn, shared=False, after_shared=False, rows=None):
                pe.wait_ge(xT_lo_ok, u + 2 if not shared or u else 1)
                for s in range(STEPS):
                    g = u * STEPS + s
                    first(g, u, s, shared, turn)
                    if s == LAG + 1:
                        if after_shared:
                            pe.wait_ge(shared_read, 2)
                        elif not isinstance(u, int) or u > 0:
                            pe.wait_ge(y_read, u * 3 - 3)
                        second(g - s, 0, shared)
                    if s > LAG:
                        second(g - LAG, s - LAG, shared)
                    elif s < LAG and (not isinstance(u, int) or u > 0):
                        second(g - LAG, STEPS + s - LAG, after_shared)
                    if rows is not None and s == 5:
                        rows(u + 1, 1 - turn)
                    if shared and u == 0 and s == 1:
                        pe.wait_ge(onehot_ok, 1)
                        oh = onehot[:, :, :, :].rearrange("p t k e -> p (t k e)")
                        w = TOPK * E
                        pe.matmul(counts, before[:, :], oh, start=True, stop=False, skip_group_check=True)
                        for j in range(T - 1):
                            later = T - 1 - j
                            src = onehot[:, j, :, :].rearrange("p k e -> p (k e)").unsqueeze(1)
                            mm = pe.matmul(counts[:, (j + 1) * w:], ones[:, :],
                                           src.broadcast_to([P, later, w]),
                                           start=False, stop=(j == T - 2), skip_group_check=True)
                        mm.then_inc(counts_mm, 1)

            def expert_rows(u, turn):
                pe.wait_ge(xT_lo_ok, u + 1)
                if isinstance(u, int):
                    pe.wait_ge(xg_in[turn], 32 * ((u + 1) // 2))
                else:
                    pe.wait_ge(xg_in[turn], (u + turn) * 16)
                transpose_rows(lambda c: xg[:, turn, c, :], 3, SLOTS)

            def shared_rows(u, turn):
                pe.wait_ge(xT_lo_ok, u + 1)
                transpose_rows(lambda c: xn[:, 4 + c, :], 4, UTOK)

            pe.wait_ge(ones_row, 2)
            unit(0, 0, shared=True)
            expert_rows(1, 1)
            unit(1, 1, after_shared=True, rows=expert_rows)
            with pe.Fori(2, E - 1, 2) as u:
                unit(u, 0, rows=expert_rows)
                unit(u + 1, 1, rows=expert_rows)
            unit(E, 0, rows=shared_rows)
            unit(E + 1, 1, shared=True)
            for s in range(STEPS - LAG, STEPS):
                second((E + 1) * STEPS + s, s, True)

            def transpose_x3(b):
                pe.wait_ge(x3n_ok, 2 * b + 2)
                if b < 2:
                    pe.wait_ge(xT_lo_ok, E + 3)
                else:
                    pe.wait_ge(x3T_lo, b - 1)
                for i in range(2):
                    for k in range(DK):
                        mm = pe.transpose(tb[b % 2][:, k * S + i * P:k * S + (i + 1) * P],
                                          xn[:, 2 * b + i, k * P:(k + 1) * P], ident[:, :])
                mm.then_inc(x3T_mm, 1)

            def gate_up(b, f):
                n = b * NG + f
                if n < RING:
                    pe.wait_ge(h_hi_ok, UNITS * STEPS)
                else:
                    pe.wait_ge(prod_ok, n - RING + 1)
                if f == 0:
                    pe.wait_ge(x3T_lo, b + 1)
                for part, first_col in enumerate((GATE0, UP0)):
                    terms = [(w, a, k) for k in range(DK)
                             for w, a in ((gw_hi, xT_hi), (gw_lo, xT_hi), (gw_hi, xT_lo))]
                    for i, (w, a, k) in enumerate(terms):
                        at = first_col + k * INTER + f * P
                        mm = pe.matmul(hb[n % RING][:, part * S:(part + 1) * S], w[:, at:at + P],
                                       a[:, b % 2, k, 0:S], start=(i == 0), stop=(i == len(terms) - 1))
                mm.then_inc(gu_mm, 1)

            def down(b, f):
                n = b * NG + f
                if n == NG:
                    pe.wait_ge(shared_read, 4)
                if f == 0 and b >= 2:
                    pe.wait_ge(x4_ok, b - 1)
                pe.wait_ge(g_lo_ok, n + 1)
                K = P if f < NG - 1 else LASTG
                for i in range(2):
                    for j, (h, w) in enumerate(((h_hi, gw_hi), (h_lo, gw_hi), (h_hi, gw_lo))):
                        at = DOWN0 + f * D
                        mm = pe.matmul(down_banks[b % 2][:, i * D:(i + 1) * D], h[0:K, n % RING, i * P:(i + 1) * P],
                                       w[0:K, at:at + D], start=(f == 0 and i == 0 and j == 0),
                                       stop=(f == NG - 1 and j == 2), skip_group_check=True)
                mm.then_inc(down_mm, 1)

            pe.wait_ge(lk, JOBS * JOPS)
            transpose_x3(0)
            for n in range(B * NG + LAG):
                if n < B * NG:
                    gate_up(n // NG, n % NG)
                if n >= LAG:
                    down((n - LAG) // NG, (n - LAG) % NG)
                if n % NG == 4 and n // NG + 1 < B:
                    transpose_x3(n // NG + 1)

        @block.scalar
        def _(act):
            def copy(dst, src, scale=1.0):
                return act.activation(dst, src, ACT.Copy, scale=scale)

            act.wait_ge(proj_mm, 3)
            for n in range(2):
                copy(kvT[:, n * 512:(n + 1) * 512], hb[n][0:H, :]).then_inc(proj_sb, 1)
            copy(kv, rb[:, :].rearrange("p (t h) -> p t h", h=H)).then_inc(proj_sb, 1)
            act.wait_ge(gate_in, 16)
            act.wait_ge(consts_ok, CONSTS)
            copy(gate_parts[:, :, 0:E], gate_w[:, :, :]).then_inc(gate_ok, 1)

            def pT_copy(b):
                act.wait_ge(pT_mm, b + 1)
                if b >= 2:
                    act.wait_ge(outT_mm, b - 1)
                copy(pT[:, b % 2, :, :], tb[b % 2][:, :].rearrange("p (k s) -> p k s", k=2)).then_inc(pT_sb, 1)

            def outT_copy(b):
                act.wait_ge(outT_mm, b + 1)
                if b >= 2:
                    act.wait_ge(sim_mm, b - 1)
                copy(outT[:, b % 2, :], yb[b % 2][0:H, 0:S]).then_inc(outT_sb, 1)

            def exps(which, b):
                for i in range(2):
                    tile = 2 * b + i
                    act.wait_ge(nmx_ok, 2 * (which * B + b) + i + 1)
                    row = exp_rows(which, b)[:, i, :]
                    act.activation(row, row, ACT.Exp, bias=nmx[:, which, tile:tile + 1],
                                   scale=rstd[:, 3, tile:tile + 1] if which else 1.0, accum_out=esum[:, which, tile:tile + 1]).then_inc(exp_ok, 1)

            def split_hi(j, slot, u):
                act.wait_ge(raw_in[slot // 3], u * 16 + 16)
                if not isinstance(j, int) or j >= STEPS:
                    act.wait_ge(mm2, j - STEPS + 1)
                copy(w_hi[:, slot, :], raw[:, slot, :]).then_inc(w_hi_ok, 1)

            def standard_sim(b):
                act.wait_ge(nmr_ok, b + 1)
                if b >= 2:
                    act.wait_ge(mv_ok[2], 2 * b - 2)
                for i in range(2):
                    tile = 2 * b + i
                    act.activation(exp_rows(0, b)[:, i, :], hb[b % RING][:, i * S:(i + 1) * S], ACT.Identity,
                                   bias=nmr[:, tile:tile + 1], scale=rstd[:, 1, tile:tile + 1]).then_inc(sm_in, 1)

            for j in range(3):
                split_hi(j, j, 0)
            pT_copy(0)
            pT_copy(1)
            for j in range(3, 5):
                split_hi(j, j, 0)
            outT_copy(0)
            pT_copy(2)
            outT_copy(1)
            pT_copy(3)
            standard_sim(0)
            outT_copy(2)
            standard_sim(1)
            outT_copy(3)
            exps(0, 0)
            split_hi(5, 5, 0)
            exps(0, 1)
            standard_sim(2)
            for n in range(4):
                act.wait_ge(qk_mm, n + 1)
                if n < 2:
                    copy(qT[:, n, :, :], tb[n][0:H, :].rearrange("p (k s) -> p k s", k=2)).then_inc(qk_sb, 1)
                else:
                    copy(kT[:, (n - 2) * 512:(n - 1) * 512], yb[n - 2][0:H, :]).then_inc(qk_sb, 1)
            standard_sim(3)
            exps(0, 2)
            for b in range(B):
                act.wait_ge(sc_mm, b + 1)
                copy(scores[:, 2 * b:2 * b + 2, :], tb[b % 2][:, :].rearrange("p (i s) -> p i s", i=2),
                     scale=float(H) ** -0.5).then_inc(sc_sb, 1)
                if b == 1:
                    exps(0, 3)
            for j in range(6, STEPS):
                split_hi(j, j, 0)

            def rows_hi(count, turn, width):
                act.wait_ge(xT_mm, count)
                for k in range(DK):
                    copy(xT_hi[:, turn, k, 0:width], tb[k][:, 0:width]).then_inc(xT_hi_ok, 1)

            for half in range(2):
                rows_hi(half + 1, half, UTOK)
                act.wait_ge(logitsT_mm, half + 1)
                copy(logitsT[:, half * UTOK:(half + 1) * UTOK], rb[0:2 * E, :]).then_inc(logitsT_sb, 1)
            act.wait_ge(ldiff_ok, 1)
            act.activation(lexp[:, :, :], ldiff[:, :, :], ACT.Exp).then_inc(lexp_ok, 1)
            act.wait_ge(bias_in, 16)

            def gelu(g, s, n, expert):
                act.wait_ge(mm1, g + 1)
                if not isinstance(g, int) or g >= RING:
                    act.wait_ge(h_lo_ok, g - RING + 1)
                    act.wait_ge(mm2, g - RING + 1)
                if s < NF:
                    bias = b1[:, expert, s:s + 1]
                    act.activation(h32[:, s % RING, 0:n], hb[s % RING][:, 0:n], ACT.Gelu, bias=bias).then_inc(h32_ok, 1)
                    act.activation(h_hi[:, s % RING, 0:n], hb[s % RING][:, 0:n], ACT.Gelu, bias=bias)\
                        .then_inc(h_hi_ok, 1)
                else:
                    act.activation(h32[0:H, s % RING, 0:n], hb[s % RING][0:H, 0:n], ACT.Gelu).then_inc(h32_ok, 1)
                    act.activation(lowrank[0:H, 0:n], hb[s % RING][0:H, 0:n], ACT.Gelu).then_inc(h_hi_ok, 1)

            def read_y(u, g, turn):
                act.wait_ge(mm2, g)
                if not isinstance(u, int) or u > 1:
                    act.wait_ge(y_out[0], u * 16 - 16)
                act.wait_ge(wsel_ok, u)
                for c in range(3):
                    if c == 2 and (not isinstance(u, int) or u > 1):
                        act.wait_ge(y_out[1], u * 16 - 16)
                    n = min(P, SLOTS - c * P)
                    copy(ysb[0:n, c, :], yb[c // 2][0:n, (c % 2) * D:(c % 2 + 1) * D],
                         scale=wsel[0:n, turn, c:c + 1]).then_inc(y_read, 1)

            def unit(u, turn, shared=False, after_shared=False, width=0):
                for s in range(STEPS):
                    g = u * STEPS + s
                    gelu(g, s, columns_of(shared), 0 if shared else u)
                    if s == 1 and not after_shared and (not isinstance(u, int) or u > 0):
                        read_y(u - 1, u * STEPS, 1 - turn)
                    if (not isinstance(u, int) or 0 < u <= E or s + AHEAD < STEPS) and (s > 2 or not u_is(u, 0)) \
                            or u_is(u, 0) and s > 2:
                        split_hi(g + AHEAD, (s + AHEAD) % STEPS, u + (s + AHEAD) // STEPS)
                    if s == 6 and width:
                        rows_hi(u + 3, 1 - turn, width)
                    if u_is(u, E + 1) and s == 7:
                        exps(1, 0)

            unit(0, 0, shared=True)
            rows_hi(3, 1, SLOTS)
            unit(1, 1, after_shared=True, width=SLOTS)
            with act.Fori(2, E - 1, 2) as u:
                unit(u, 0, width=SLOTS)
                unit(u + 1, 1, width=SLOTS)
            unit(E, 0, width=UTOK)
            unit(E + 1, 1, shared=True)
            def x3T_copy(b):
                act.wait_ge(x3T_mm, b + 1)
                if b >= 2:
                    act.wait_ge(gu_mm, (b - 1) * NG)
                copy(xT_hi[:, b % 2, :, 0:S], tb[b % 2][:, :].rearrange("p (k s) -> p k s", k=DK)).then_inc(x3T_hi, 1)

            x3T_copy(0)
            exps(1, 1)
            for n in range(B * NG):
                b, f = n // NG, n % NG
                if n == 8:
                    exps(1, 2)
                    exps(1, 3)
                act.wait_ge(gu_mm, n + 1)
                act.activation(h32[:, n % RING, S:2 * S], hb[n % RING][:, 0:S], ACT.Silu).then_inc(silu_ok, 1)
                if f == 4 and b + 1 < B:
                    x3T_copy(b + 1)

        @block.vector
        def _(dve):
            n_bst = {"n": 0}
            n_sm = {"n": 0}

            def stats(stage, tile, src):
                dve.bn_stats(bst[:, tile, :], src).then_inc(bst_ok, 1)
                n_bst["n"] += 1
                dve.wait_ge(bst_ok, n_bst["n"])
                dve.bn_aggr(mv[:, stage, tile, :], bst[:, tile, :]).then_inc(mv_ok[stage], 1)

            def normalise(stage, tile, dst, src, done):
                dve.tensor_scalar(dst, src, mv[:, stage, tile, 0:1], rstd[:, stage, tile:tile + 1],
                                  ALU.subtract, ALU.mult).then_inc(done, 1)

            def own(ins):
                ins.then_inc(sm_step, 1)
                n_sm["n"] += 1
                dve.wait_ge(sm_step, n_sm["n"])

            def lookup(n, before_job, loads, at, w):
                if n == 0:
                    dve.wait_ge(idx_in, loads)
                    dve.wait_ge(lut_in, 16)
                    dve.tensor_copy(idxb[:, 0:w], idx32[:, 0:w]).then_inc(lk, 1)
                    dve.wait_ge(lk, before_job + 1)
                    dve.tensor_scalar(lacc[:, 0:w], idxb[:, 0:w], 0.0, lut[:, 0:1], ALU.is_equal, ALU.mult).then_inc(lk, 1)
                elif n < LUTN:
                    dve.tensor_scalar(hit[:, n % 2, 0:w], idxb[:, 0:w], float(n), None, ALU.is_equal).then_inc(lk, 1)
                    dve.wait_ge(lk, before_job + 2 * n + 1)
                    dve.scalar_tensor_tensor(out=lacc[:, 0:w], in0=hit[:, n % 2, 0:w], scalar=lut[:, n:n + 1],
                                             in1=lacc[:, 0:w], op0=ALU.mult, op1=ALU.add).then_inc(lk, 1)
                elif n == LUTN:
                    dve.wait_ge(lk, before_job + 2 * LUTN)
                    dve.tensor_copy(gw_hi[:, at], lacc[:, 0:w]).then_inc(lk, 1)
                else:
                    dve.wait_ge(lk, before_job + 2 * LUTN + 1)
                    dve.tensor_tensor(gw_lo[:, at], lacc[:, 0:w], gw_hi[:, at].bitcast(F32), ALU.subtract)\
                        .then_inc(lk, 1)

            for b in range(B):
                dve.wait_ge(x_in[b], 16)
                for tile in (2 * b, 2 * b + 1):
                    stats(0, tile, x[:, tile, :])
            for b in range(B):
                dve.wait_ge(rstd_ok[0], b + 1)
                for tile in (2 * b, 2 * b + 1):
                    normalise(0, tile, xn[:, tile, 0:D], x[:, tile, :], p_ok)
            dve.wait_ge(gate_ok, 1)
            dve.tensor_tensor(gate_parts[:, :, E:2 * E], gate_w[:, :, :], gate_parts[:, :, 0:E].bitcast(F32),
                              ALU.subtract).then_inc(gate_ok, 1)
            dve.wait_ge(ln_in, 32)

            def sim_stats(b):
                dve.wait_ge(sim_mm, b + 1)
                for i in range(2):
                    stats(1, 2 * b + i, hb[b % RING][:, i * S:(i + 1) * S])

            def offsets(b):
                ts = slice(2 * b, 2 * b + 2)
                dve.wait_ge(rstd_ok[1], b + 1)
                dve.scalar_tensor_tensor(out=nmr[:, ts], in0=mv[:, 1, ts, 0], scalar=-1.0,
                                         in1=rstd[:, 1, ts], op0=ALU.mult, op1=ALU.mult).then_inc(nmr_ok, 1)

            def sim_rows(b):
                dve.wait_ge(gain_ok, b + 1)
                for i in range(2):
                    col = slice(2 * b + i, 2 * b + i + 1)
                    row = exp_rows(0, b)[:, i, :]
                    own(dve.tensor_tensor_reduce(row, row, beta[:, :], 1.0, LOWEST, ALU.add, ALU.max, mx[:, 0, col]))
                    dve.tensor_scalar(nmx[:, 0, col], mx[:, 0, col], -1.0, 0.0, ALU.mult, ALU.add).then_inc(nmx_ok, 1)

            def add_probs(which, b, stage, rows=(0, 1)):
                ts = slice(2 * b, 2 * b + 2)
                dve.wait_ge(exp_ok, 2 * (which * B + b) + 2)
                if rows[0] == 0:
                    own(dve.reciprocal(rsum[:, which, ts], esum[:, which, ts]))
                for i in rows:
                    tile = 2 * b + i
                    own(dve.scalar_tensor_tensor(out=x[:, tile, :], in0=exp_rows(which, b)[:, i, :],
                                                 scalar=rsum[:, which, tile:tile + 1], in1=x[:, tile, :],
                                                 op0=ALU.mult, op1=ALU.add))
                    stats(stage, tile, x[:, tile, :])

            def norm_x(stage, b, done):
                dve.wait_ge(rstd_ok[stage], b + 1)
                for tile in (2 * b, 2 * b + 1):
                    normalise(stage, tile, xn[:, tile, 0:D], x[:, tile, :], done)

            for n in range(EARLY):
                lookup(n, 0, 16, slice(0, JOB_W[0]), JOB_W[0])
            sim_stats(0)
            offsets(0)
            sim_stats(1)
            offsets(1)
            sim_rows(0)
            sim_stats(2)
            offsets(2)
            sim_rows(1)
            add_probs(0, 0, 2)
            sim_stats(3)
            offsets(3)
            add_probs(0, 1, 2)
            sim_rows(2)
            norm_x(2, 0, xn_ok)
            norm_x(2, 1, xn_ok)
            sim_rows(3)
            add_probs(0, 2, 2)
            add_probs(0, 3, 2)
            norm_x(2, 2, xn_ok)
            norm_x(2, 3, xn_ok)

            def rows_lo(count, turn, width):
                for k in range(DK):
                    dve.wait_ge(xT_hi_ok, (count - 1) * DK + k + 1)
                    ins = dve.tensor_tensor(xT_lo[:, turn, k, 0:width], tb[k][:, 0:width],
                                            xT_hi[:, turn, k, 0:width].bitcast(F32), ALU.subtract)
                ins.then_inc(xT_lo_ok, 1)

            rows_lo(1, 0, UTOK)
            rows_lo(2, 1, UTOK)

            n_rt = {"n": 0}

            def rts(ins):
                ins.then_inc(rt, 1)
                n_rt["n"] += 1

            def rt_wait():
                dve.wait_ge(rt, n_rt["n"])

            dve.wait_ge(logits_mm, 1)
            dve.wait_ge(consts_ok, CONSTS)
            rts(dve.tensor_copy(logits[:, :, :], parts[:, :, 0, :]))
            rt_wait()
            rts(dve.tensor_tensor(logits[:, :, :], logits[:, :, :], parts[:, :, 1, :], ALU.add))
            rt_wait()
            for tile in range(T):
                rts(dve.max(top8[:, tile, :], logits[:, tile, :]))
            rt_wait()
            for tile in range(T):
                rts(dve.max_index(topi[:, tile, :], top8[:, tile, :], logits[:, tile, :]))
            rts(dve.tensor_tensor(ldiff[:, :, 0:E], logits[:, :, :], top8[:, :, 0:1].broadcast_to([P, T, E]), ALU.subtract))
            dve.tensor_tensor(ldiff[:, :, E:E + TOPK], top8[:, :, 0:TOPK],
                              top8[:, :, 0:1].broadcast_to([P, T, TOPK]), ALU.subtract).then_inc(ldiff_ok, 1)
            rt_wait()
            rts(dve.tensor_copy(topf[:, :, :], topi[:, :, 0:TOPK]))
            rt_wait()
            shape = [P, T, TOPK, E]
            dve.tensor_tensor(onehot[:, :, :, :], topf[:, :, :].unsqueeze(3).broadcast_to(shape),
                              expert_no[:, :].unsqueeze(1).unsqueeze(1).broadcast_to(shape), ALU.is_equal)\
                .then_inc(onehot_ok, 1)
            for k in range(TOPK):
                rts(dve.tensor_scalar(base[:, :, k:k + 1], topf[:, :, k:k + 1], float(SLOTS), float(k * CAP),
                                      ALU.mult, ALU.add))
            dve.wait_ge(lexp_ok, 1)
            rts(dve.tensor_reduce(lrs[:, :], lexp[:, :, 0:E], AX.X, ALU.add))
            rt_wait()
            rts(dve.reciprocal(lrs[:, :], lrs[:, :]))
            rt_wait()
            dve.tensor_tensor(xn[:, :, D:ROW], lexp[:, :, E:E + TOPK], lrs[:, :].unsqueeze(2).broadcast_to([P, T, TOPK]),
                              ALU.mult).then_inc(wtok_ok, 1)
            def route():
                dve.wait_ge(counts_mm, 1)
                dve.wait_ge(onehot_ok, 1)
                rts(dve.tensor_tensor(poh[:, :, :, :], onehot[:, :, :, :],
                                      counts.rearrange("p (t k e) -> p t k e", t=T, k=TOPK), ALU.mult))
                rt_wait()
                rts(dve.tensor_reduce(pos[:, :, :], poh[:, :, :, :], AX.X, ALU.add))
                rt_wait()
                rts(dve.tensor_scalar(over[:, :, :], pos[:, :, :], float(CAP), BIG, ALU.is_ge, ALU.mult))
                rts(dve.tensor_tensor(put_f[:, :, :], pos[:, :, :], base[:, :, :], ALU.add))
                rt_wait()
                rts(dve.tensor_tensor(put_f[:, :, :], put_f[:, :, :], over[:, :, :], ALU.add))
                rt_wait()
                dve.tensor_copy(put_i[:, :, :], put_f[:, :, :]).then_inc(put_ok, 1)
                rts(dve.tensor_scalar(get_f[:, :, :], put_f[:, :, :], float(E * SLOTS), None, ALU.min))
                rt_wait()
                dve.tensor_copy(get_i[:, :, :], get_f[:, :, :]).then_inc(get_ok, 1)

            def build_masks():
                dve.wait_ge(mask_in, 32)
                for b in range(B):
                    own(dve.tensor_tensor(mask_add[:, 2 * b:2 * b + 2, :], mask_u8[:, :, :],
                                          pad_u8[:, b, :].unsqueeze(1).broadcast_to([P, 2, S]), ALU.max))
                own(dve.tensor_reduce(dead[:, :], mask_add[:, :, :], AX.X, ALU.min))
                own(dve.tensor_scalar(dead[:, :], dead[:, :], 3.0e38, 1.0e10, ALU.mult, ALU.mult))
                own(dve.tensor_tensor(dead[:, :], dead[:, :], dead[:, :], ALU.subtract))
                own(dve.tensor_scalar(mask_add[:, :, :], mask_add[:, :, :], -1.0e36, None, ALU.mult))

            def lo(g, s, n):
                dve.wait_ge(h32_ok, g + 1)
                dve.wait_ge(h_hi_ok, g + 1)
                r = s % RING
                if s < NF:
                    dve.tensor_tensor(h_lo[:, r, 0:n], h32[:, r, 0:n], h_hi[:, r, 0:n].bitcast(F32), ALU.subtract)\
                        .then_inc(h_lo_ok, 1)
                else:
                    dve.tensor_tensor(lowrank[RANK:H, 0:n], h32[RANK:H, r, 0:n], lowrank[RANK:H, 0:n].bitcast(F32),
                                      ALU.subtract).then_inc(h_lo_ok, 1)

            def weights_of(u, turn):
                if not isinstance(u, int) or u > 1:
                    dve.wait_ge(y_read, u * 3 - 6)
                    dve.wait_ge(wsel_ok, u - 1)
                dve.wait_ge(xg_in[turn], u * 16 + 16 if turn else u * 16)
                dve.tensor_tensor(wrow[:, :, :], xg[:, turn, :, D:ROW], round_of[:, :, :], ALU.mult).then_inc(wr_ok, 1)
                dve.wait_ge(wr_ok, u)
                dve.tensor_reduce(wsel[:, turn, :], wrow[:, :, :], AX.X, ALU.add).then_inc(wsel_ok, 1)

            def unit(u, turn, shared=False, after_shared=False, width=0, extra=None):
                for s in range(STEPS):
                    if s == 6 and u_is(u, E + 1):
                        combined(0)
                    lo(u * STEPS + s, s, columns_of(shared))
                    if s == 1 and after_shared:
                        add_shared(0)
                    if s == 6 and width:
                        rows_lo(u + 3, 1 - turn, width)
                        if width == SLOTS:
                            weights_of(u + 1, 1 - turn)
                    if extra is not None:
                        extra(s)

            def add_shared(half):
                dve.wait_ge(mm2, STEPS if half == 0 else UNITS * STEPS)
                for i in range(2):
                    ts = slice(4 * half + 2 * i, 4 * half + 2 * i + 2)
                    dve.scalar_tensor_tensor(out=x[:, ts, :], in0=yb[i][:, :].rearrange("p (c d) -> p c d", c=2),
                                             scalar=0.2, in1=x[:, ts, :], op0=ALU.mult, op1=ALU.add)\
                        .then_inc(shared_read, 1)

            def combined(b):
                for tile in (2 * b, 2 * b + 1):
                    dve.wait_ge(gath_in[tile], 16 * TOPK)
                    stats(3, tile, x[:, tile, :])

            def attend(b):
                for i in range(2):
                    tile = 2 * b + i
                    own(dve.scalar_tensor_tensor(out=exp_rows(1, b)[:, i, :], in0=x[:, tile, :],
                                                 scalar=mv[:, 3, tile, 0:1], in1=scores[:, tile, :],
                                                 op0=ALU.subtract, op1=ALU.mult))
                ts = slice(2 * b, 2 * b + 2)
                for i in range(2):
                    col = slice(2 * b + i, 2 * b + i + 1)
                    row = exp_rows(1, b)[:, i, :]
                    own(dve.tensor_tensor_reduce(row, row, mask_add[:, 2 * b + i, :], 1.0, LOWEST, ALU.add, ALU.max,
                                                 mx[:, 1, col]))
                    own(dve.tensor_scalar(mx[:, 1, col], mx[:, 1, col], -1.0, dead[:, col], ALU.mult, ALU.add))
                dve.wait_ge(rstd_ok[3], b + 1)
                dve.tensor_tensor(nmx[:, 1, ts], mx[:, 1, ts], rstd[:, 3, ts], ALU.mult).then_inc(nmx_ok, 2)

            def w_lo_share(s):
                if s >= STEPS - AHEAD:
                    j = s + AHEAD
                    dve.wait_ge(w_hi_ok, j + 1)
                    dve.wait_ge(w_lo_ok, j)
                    dve.tensor_tensor(w_lo[:, j % STEPS, :], raw[:, j % STEPS, :],
                                      w_hi[:, j % STEPS, :].bitcast(F32), ALU.subtract).then_inc(w_lo_ok, 1)

            def unit0_extra(s):
                w_lo_share(s)
                if s == 0:
                    route()
                lookup(EARLY + s, 0, 16, slice(0, JOB_W[0]), JOB_W[0])

            def unit1_extra(s):
                if EARLY + STEPS + s < LUTN + 2:
                    lookup(EARLY + STEPS + s, 0, 16, slice(0, JOB_W[0]), JOB_W[0])
                if s == STEPS - 2:
                    build_masks()

            def unit8_extra(s):
                for n in (2 * s, 2 * s + 1):
                    lookup(n, 4 * JOPS, 16 * JOBS, slice(JOB_AT[4], LUTW), JOB_W[4])

            def tail(s):
                if s == 6:
                    attend(0)
                if s == 7:
                    combined(1)
                    add_probs(1, 0, 4)

            unit(0, 0, shared=True, extra=unit0_extra)
            rows_lo(3, 1, SLOTS)
            weights_of(1, 1)
            unit(1, 1, after_shared=True, width=SLOTS, extra=unit1_extra)
            with dve.Fori(2, E - 1, 2) as u:
                at = bass.ds(u * (JOB_W[1] // 2) + LOOP_AT, JOB_W[1])

                def pair(first_n):
                    return lambda s: lookup(first_n + s, u * (JOPS // 2), u * 8 + 16, at, JOB_W[1])

                unit(u, 0, width=SLOTS, extra=pair(0))
                unit(u + 1, 1, width=SLOTS, extra=pair(STEPS))
            unit(E, 0, width=UTOK, extra=unit8_extra)
            dve.wait_ge(shared_read, 2)
            unit(E + 1, 1, shared=True, extra=tail)
            norm_x(4, 0, x3n_ok)
            attend(1)

            def x3T_split(b):
                dve.wait_ge(x3T_hi, b + 1)
                dve.tensor_tensor(xT_lo[:, b % 2, :, 0:S], tb[b % 2][:, :].rearrange("p (k s) -> p k s", k=DK),
                                  xT_hi[:, b % 2, :, 0:S].bitcast(F32), ALU.subtract).then_inc(x3T_lo, 1)

            def finish(b):
                dve.wait_ge(down_mm, (b + 1) * NG)
                ts = slice(2 * b, 2 * b + 2)
                dve.tensor_tensor(x[:, ts, :], x[:, ts, :], down_banks[b % 2][:, :].rearrange("p (c d) -> p c d", c=2),
                                  ALU.add).then_inc(x4_ok, 1)

            x3T_split(0)
            for n in range(B * NG):
                b, f = n // NG, n % NG
                r = n % RING
                dve.wait_ge(silu_ok, n + 1)
                if n >= RING:
                    dve.wait_ge(down_mm, n - RING + 1)
                dve.tensor_tensor(h_hi[:, r, 0:S], h32[:, r, S:2 * S], hb[r][:, S:2 * S], ALU.mult)
                dve.tensor_tensor(h32[:, r, 0:S], h32[:, r, S:2 * S], hb[r][:, S:2 * S], ALU.mult).then_inc(prod_ok, 1)
                if n == 0:
                    add_probs(1, 1, 4, (0,))
                elif n == 1:
                    add_probs(1, 1, 4, (1,))
                elif n == 2:
                    for tile in range(4, T):
                        dve.wait_ge(gath_in[tile], 16 * TOPK)
                    add_shared(1)
                    norm_x(4, 1, x3n_ok)
                elif n == 3:
                    dve.wait_ge(shared_read, 4)
                    combined(2)
                elif n == 4:
                    combined(3)
                elif n == 5:
                    attend(2)
                elif n == 6:
                    attend(3)
                elif n == 8:
                    add_probs(1, 2, 4)
                elif n == 9:
                    norm_x(4, 2, x3n_ok)
                elif n == 11:
                    add_probs(1, 3, 4, (0,))
                elif n == 12:
                    add_probs(1, 3, 4, (1,))
                elif n == 15:
                    norm_x(4, 3, x3n_ok)
                if f == 4 and b + 1 < B:
                    x3T_split(b + 1)
                if f == 2 and b > 0:
                    finish(b - 1)
            finish(B - 1)


def kernel(**inputs):
    import numpy as np
    import concourse.bacc as bacc
    from concourse.bass_utils import run_bass_kernel_spmd

    def arr(name):
        return np.ascontiguousarray(inputs[name])

    def lanes(a, n=P):
        return np.ascontiguousarray(np.broadcast_to(a, (n, *a.shape)))

    def stream(w1, w2, wd, wu, b2):
        first = w1.reshape(DK, P, NF, P).transpose(1, 2, 0, 3).reshape(P, NF, DK * P)
        second = w2.reshape(NF, P, D).transpose(1, 0, 2)
        low = np.concatenate([wd] * (P // RANK), axis=1).reshape(DK, P, P).transpose(1, 0, 2).reshape(P, 1, DK * P)
        up = np.concatenate([wu, wu, b2[None, :], np.zeros((P - 2 * RANK - 1, D), w1.dtype)])[:, None, :]
        main = np.concatenate([first, second], axis=2)
        return np.concatenate([main, np.concatenate([low, up], axis=2)], axis=1).reshape(P, STEPS * WSTEP)

    ffn = {n: arr("L0_ffn_" + n) for n in
           ("w1", "b1", "w2", "b2", "wd", "wu", "sw1", "sb1", "sw2", "sb2", "swd", "swu", "gate_w")}
    wpack = np.stack([stream(ffn["sw1"], ffn["sw2"], ffn["swd"], ffn["swu"], ffn["sb2"])]
                     + [stream(*(ffn[n][e] for n in ("w1", "w2", "wd", "wu", "b2"))) for e in range(E)])
    b1 = np.concatenate([ffn["sb1"][None, :], ffn["b1"]]).reshape(E + 1, NF, P).transpose(2, 0, 1)
    one = np.ones((1, NTOK), np.float32)
    ctxT = np.concatenate([arr("ctx_512").reshape(NTOK, H).T, one])
    projw = np.stack([np.concatenate([arr(w).T, arr(b)[None, :]]) for w, b in
                      (("L0_xattn_W_k", "L0_xattn_b_k"), ("L1_xattn_Wq", "L1_xattn_bq"), ("L1_xattn_Wk", "L1_xattn_bk"))],
                     axis=1)
    gate, up, down = (arr("L1_ffn_" + n + "_idx") for n in ("gate", "up", "down"))
    down_t = np.concatenate([down.T, np.zeros((NG * P - INTER, D), down.dtype)])
    idx = np.concatenate([a.T.reshape(DK, P, INTER).transpose(1, 0, 2).reshape(P, DK * INTER) for a in (gate, up)]
                         + [down_t.reshape(NG, P, D).transpose(1, 0, 2).reshape(P, NG * D)], axis=1)
    arrays = {
        "x": arr("x"), "ctxT": ctxT, "projw": projw,
        "gamma": lanes(arr("L0_xattn_ln_gamma")), "beta": lanes(arr("L0_xattn_ln_beta")),
        "gate_w": ffn["gate_w"], "b1": b1, "wpack": wpack,
        "idx": idx, "lut": lanes(arr("L1_ffn_lut")),
        "mask": arr("mask_SxS2_bk1"), "pad": lanes(arr("mask_BxS2_bf0")),
    }
    arrays = {n + "_dram": np.ascontiguousarray(a) for n, a in arrays.items()}
    nc = bacc.Bacc("TRN2", target_bir_lowering=False, num_devices=1)
    tensors = {n[:-5]: nc.dram_tensor(n, a.shape, mybir.dt.from_np(a.dtype), kind="ExternalInput").ap()
               for n, a in arrays.items()}
    tensors["xbuf"] = nc.dram_tensor("xbuf_dram", (E, SLOTS, ROW), F32).ap()
    tensors["ybuf"] = nc.dram_tensor("ybuf_dram", (E * SLOTS + 1, D), F32).ap()
    tensors["out"] = nc.dram_tensor("out_dram", (B, S, D), F32, kind="ExternalOutput").ap()
    program(nc, tensors)
    return run_bass_kernel_spmd(nc, [arrays], core_ids=[0]).results[0]["out_dram"]
```
